# Optimizing a Trainium2 kernel written in Bass

```python
import numpy as np
import jax
import jax.numpy as jnp

def _softmax(x, axis=-1):
    return jax.nn.softmax(x, axis=axis)

def _gelu(x):
    return jax.nn.gelu(x, approximate=True)

def _silu(x):
    return jax.nn.silu(x)

def _sigmoid(x):
    return jax.nn.sigmoid(x)

def _layernorm(x, axis=-1, eps=1e-05):
    m = jnp.mean(x, axis=axis, keepdims=True)
    v = jnp.var(x, axis=axis, keepdims=True)
    return (x - m) / jnp.sqrt(v + eps)

def _scatter_add(tgt, idx, src, axis=0):
    return tgt.at[idx].add(src)

def _segment_sum(src, seg, n):
    return jax.ops.segment_sum(src, seg, n)
kernel_name = 'mk_dlrm_tower_d1_rec_r8_76a6b3'

def setup_inputs(seed: int=0):
    np.random.seed(seed)
    _w = jnp.asarray

    def _rec_inputs():
        import jax
        import jax.numpy as jnp
        _tk = jax.random.key(seed)
        ids = jnp.stack([jax.random.randint(jax.random.fold_in(_tk, 200 + f), (2048,), 0, v, jnp.int32) for f, v in enumerate([125000, 1250, 1250, 1250, 1250, 1000, 1250, 1250, 1250, 12500, 1000, 1250, 1000, 1000, 12500, 1250, 1000, 1000, 12500, 12500, 1000, 12500, 12500, 1250, 1250, 12500])], axis=1)
        tbl_0 = 0.05 * jax.random.normal(jax.random.fold_in(_tk, 500 + 0), (125000, 128), jnp.float32)
        tbl_1 = 0.05 * jax.random.normal(jax.random.fold_in(_tk, 500 + 1), (1250, 128), jnp.float32)
        tbl_2 = 0.05 * jax.random.normal(jax.random.fold_in(_tk, 500 + 2), (1250, 128), jnp.float32)
        tbl_3 = 0.05 * jax.random.normal(jax.random.fold_in(_tk, 500 + 3), (1250, 128), jnp.float32)
        tbl_4 = 0.05 * jax.random.normal(jax.random.fold_in(_tk, 500 + 4), (1250, 128), jnp.float32)
        tbl_5 = 0.05 * jax.random.normal(jax.random.fold_in(_tk, 500 + 5), (1000, 128), jnp.float32)
        tbl_6 = 0.05 * jax.random.normal(jax.random.fold_in(_tk, 500 + 6), (1250, 128), jnp.float32)
        tbl_7 = 0.05 * jax.random.normal(jax.random.fold_in(_tk, 500 + 7), (1250, 128), jnp.float32)
        tbl_8 = 0.05 * jax.random.normal(jax.random.fold_in(_tk, 500 + 8), (1250, 128), jnp.float32)
        tbl_9 = 0.05 * jax.random.normal(jax.random.fold_in(_tk, 500 + 9), (12500, 128), jnp.float32)
        tbl_10 = 0.05 * jax.random.normal(jax.random.fold_in(_tk, 500 + 10), (1000, 128), jnp.float32)
        tbl_11 = 0.05 * jax.random.normal(jax.random.fold_in(_tk, 500 + 11), (1250, 128), jnp.float32)
        tbl_12 = 0.05 * jax.random.normal(jax.random.fold_in(_tk, 500 + 12), (1000, 128), jnp.float32)
        tbl_13 = 0.05 * jax.random.normal(jax.random.fold_in(_tk, 500 + 13), (1000, 128), jnp.float32)
        tbl_14 = 0.05 * jax.random.normal(jax.random.fold_in(_tk, 500 + 14), (12500, 128), jnp.float32)
        tbl_15 = 0.05 * jax.random.normal(jax.random.fold_in(_tk, 500 + 15), (1250, 128), jnp.float32)
        tbl_16 = 0.05 * jax.random.normal(jax.random.fold_in(_tk, 500 + 16), (1000, 128), jnp.float32)
        tbl_17 = 0.05 * jax.random.normal(jax.random.fold_in(_tk, 500 + 17), (1000, 128), jnp.float32)
        tbl_18 = 0.05 * jax.random.normal(jax.random.fold_in(_tk, 500 + 18), (12500, 128), jnp.float32)
        tbl_19 = 0.05 * jax.random.normal(jax.random.fold_in(_tk, 500 + 19), (12500, 128), jnp.float32)
        tbl_20 = 0.05 * jax.random.normal(jax.random.fold_in(_tk, 500 + 20), (1000, 128), jnp.float32)
        tbl_21 = 0.05 * jax.random.normal(jax.random.fold_in(_tk, 500 + 21), (12500, 128), jnp.float32)
        tbl_22 = 0.05 * jax.random.normal(jax.random.fold_in(_tk, 500 + 22), (12500, 128), jnp.float32)
        tbl_23 = 0.05 * jax.random.normal(jax.random.fold_in(_tk, 500 + 23), (1250, 128), jnp.float32)
        tbl_24 = 0.05 * jax.random.normal(jax.random.fold_in(_tk, 500 + 24), (1250, 128), jnp.float32)
        tbl_25 = 0.05 * jax.random.normal(jax.random.fold_in(_tk, 500 + 25), (12500, 128), jnp.float32)
        _rk = jax.random.fold_in(_tk, 7)
        r_dense_output = -0.000520686 + 1.00062 * jax.random.normal(jax.random.fold_in(_rk, 101), (2048, 128), jnp.float32)
        W_top1 = 0.0405887 * jax.random.normal(jax.random.fold_in(_tk, 801), (607, 512), jnp.float32)
        W_top2 = 0.0441942 * jax.random.normal(jax.random.fold_in(_tk, 802), (512, 256), jnp.float32)
        W_top3 = 0.0625 * jax.random.normal(jax.random.fold_in(_tk, 803), (256, 1), jnp.float32)
        b_top1 = jnp.zeros((512,), jnp.float32)
        b_top2 = jnp.zeros((256,), jnp.float32)
        return (r_dense_output, ids, tbl_0, tbl_1, tbl_2, tbl_3, tbl_4, tbl_5, tbl_6, tbl_7, tbl_8, tbl_9, tbl_10, tbl_11, tbl_12, tbl_13, tbl_14, tbl_15, tbl_16, tbl_17, tbl_18, tbl_19, tbl_20, tbl_21, tbl_22, tbl_23, tbl_24, tbl_25, W_top1, b_top1, W_top2, b_top2, W_top3)
    r_dense_output, ids, tbl_0, tbl_1, tbl_2, tbl_3, tbl_4, tbl_5, tbl_6, tbl_7, tbl_8, tbl_9, tbl_10, tbl_11, tbl_12, tbl_13, tbl_14, tbl_15, tbl_16, tbl_17, tbl_18, tbl_19, tbl_20, tbl_21, tbl_22, tbl_23, tbl_24, tbl_25, W_top1, b_top1, W_top2, b_top2, W_top3 = _rec_inputs()

    def _L0_rec_setup():
        import jax, jax.numpy as jnp
        import numpy as np
        B, NUM_SPARSE, D = (2048, 26, 128)
        key = jax.random.key(seed)
        k1, k2 = jax.random.split(key)
        dense_output = jax.random.normal(k1, (B, D), dtype=jnp.float32)
        embeddings = jax.random.normal(k2, (B, NUM_SPARSE, D), dtype=jnp.float32)
        return {'dense_output': dense_output, 'embeddings': embeddings}
    _L0_rec_all = _L0_rec_setup()
    _L0_rec_in = {k: v for k, v in _L0_rec_all.items() if k in ()}
    del _L0_rec_all
    return {'r_dense_output': r_dense_output, 'ids': ids, 'tbl_0': tbl_0, 'tbl_1': tbl_1, 'tbl_2': tbl_2, 'tbl_3': tbl_3, 'tbl_4': tbl_4, 'tbl_5': tbl_5, 'tbl_6': tbl_6, 'tbl_7': tbl_7, 'tbl_8': tbl_8, 'tbl_9': tbl_9, 'tbl_10': tbl_10, 'tbl_11': tbl_11, 'tbl_12': tbl_12, 'tbl_13': tbl_13, 'tbl_14': tbl_14, 'tbl_15': tbl_15, 'tbl_16': tbl_16, 'tbl_17': tbl_17, 'tbl_18': tbl_18, 'tbl_19': tbl_19, 'tbl_20': tbl_20, 'tbl_21': tbl_21, 'tbl_22': tbl_22, 'tbl_23': tbl_23, 'tbl_24': tbl_24, 'tbl_25': tbl_25, 'W_top1': W_top1, 'b_top1': b_top1, 'W_top2': W_top2, 'b_top2': b_top2, 'W_top3': W_top3}

def reference(r_dense_output, ids, tbl_0, tbl_1, tbl_2, tbl_3, tbl_4, tbl_5, tbl_6, tbl_7, tbl_8, tbl_9, tbl_10, tbl_11, tbl_12, tbl_13, tbl_14, tbl_15, tbl_16, tbl_17, tbl_18, tbl_19, tbl_20, tbl_21, tbl_22, tbl_23, tbl_24, tbl_25, W_top1, b_top1, W_top2, b_top2, W_top3):
    import jax
    import jax.numpy as jnp

    def _L0_rec_ref(dense_output, embeddings):
        import jax, jax.numpy as jnp
        import numpy as np
        B, NUM_SPARSE, D = (2048, 26, 128)
        combined = jnp.concatenate([dense_output[:, None, :], embeddings], axis=1)
        interactions = jnp.einsum('bfd,bgd->bfg', combined, combined)
        F = combined.shape[1]
        iu, ju = jnp.triu_indices(F, k=1)
        interactions_flat = interactions[:, iu, ju]
        return jnp.concatenate([dense_output, interactions_flat], axis=1)
    e = jnp.stack([tbl_0[ids[:, 0]], tbl_1[ids[:, 1]], tbl_2[ids[:, 2]], tbl_3[ids[:, 3]], tbl_4[ids[:, 4]], tbl_5[ids[:, 5]], tbl_6[ids[:, 6]], tbl_7[ids[:, 7]], tbl_8[ids[:, 8]], tbl_9[ids[:, 9]], tbl_10[ids[:, 10]], tbl_11[ids[:, 11]], tbl_12[ids[:, 12]], tbl_13[ids[:, 13]], tbl_14[ids[:, 14]], tbl_15[ids[:, 15]], tbl_16[ids[:, 16]], tbl_17[ids[:, 17]], tbl_18[ids[:, 18]], tbl_19[ids[:, 19]], tbl_20[ids[:, 20]], tbl_21[ids[:, 21]], tbl_22[ids[:, 22]], tbl_23[ids[:, 23]], tbl_24[ids[:, 24]], tbl_25[ids[:, 25]]], axis=1)
    z = _L0_rec_ref(r_dense_output, e)
    z = z.reshape(z.shape[0], -1)
    h = jnp.concatenate([z, r_dense_output], axis=1)
    h = jnp.maximum(h @ W_top1 + b_top1, 0.0)
    h = jnp.maximum(h @ W_top2 + b_top2, 0.0)
    y = h @ W_top3
    return y

_drawn_inputs = setup_inputs


def setup_inputs(seed=0):
    import zlib

    import numpy as np

    out = dict(_drawn_inputs(seed))
    spreads = {'b_top1': (0.0, 0.1), 'b_top2': (0.0, 0.1)}
    factors = {}
    for name, (base, spread) in spreads.items():
        noise = np.random.default_rng([zlib.crc32(name.encode()), seed]).standard_normal(out[name].shape)
        drawn = base * np.exp(spread * noise) if base else spread * noise
        out[name] = jnp.asarray(drawn.astype(out[name].dtype))
    for name, factor in factors.items():
        out[name] = (out[name] * factor).astype(out[name].dtype)
    return out
```

```python
from contextlib import ExitStack

import concourse.bass as bass
from concourse import mybir

F32 = mybir.dt.float32
F32R = mybir.dt.float32r
F16 = mybir.dt.float16
I32 = mybir.dt.int32
ALU = mybir.AluOpType
ACT = mybir.ActivationFunctionType

P = 128
CHUNK = 256
TILES = CHUNK // P
QUAD = 32
ROWS_QUAD = P // 4
PAIRED = 2
OH_BUFS = 4
HOT_AHEAD = 2
HOT_TABLES = 6


def uniform_groups(features, most):
    groups = []
    for f in features:
        g = groups[-1] if groups else None
        if g and len(g) < most and (len(g) == 1 or f - g[-1] == g[-1] - g[-2]):
            g.append(f)
        else:
            groups.append([f])
    return groups


def stepped(group):
    step = group[1] - group[0] if len(group) > 1 else 1
    return slice(group[0], group[-1] + 1, step)


def build(nc, dense, ids, ids_t, tables, W1, b1, W2, b2, W3, scratch, out):
    B, D = dense.shape
    F = len(tables) + 1
    HID1, HID2 = W2.shape
    NPAIR = F * (F - 1) // 2
    CHUNKS = B // CHUNK
    KP = -(-NPAIR // P)
    KD = KP
    M1, M2 = HID1 // P, HID2 // P
    assert D == P and W1.shape[0] == D + NPAIR + D and F <= QUAD

    hot = sorted(sorted(range(len(tables)), key=lambda t: tables[t].shape[0])[:HOT_TABLES])
    VOCAB = tables[hot[0]].shape[0]
    CK = -(-VOCAB // P)
    VP = VOCAB // CK
    assert all(tables[t].shape[0] == VP * CK for t in hot) and VOCAB <= 2048
    gathered = [t for t in range(len(tables)) if t not in hot]
    NGATH = len(gathered)
    slot_of = {t + 1: n for n, t in enumerate(gathered)}
    groups = uniform_groups([0] + [t + 1 for t in gathered], 4)
    NGRP = len(groups)
    units = [hot[n:n + PAIRED] for n in range(0, len(hot), PAIRED)]
    UNITS = len(units)
    STEPS = UNITS * CK
    GB = 4
    GBANKS = ROWS_QUAD // GB
    FM = F - 1
    ACT_QUADS, DVE_QUADS = (0, 1), (2, 3)

    reads = []
    base = 0
    for f in range(F - 1):
        g = f + 1
        while g < F:
            row = base + g - f - 1
            n = min(F - g, P - row % P)
            reads.append((f, g, n, row // P, row % P))
            g += n
        base += F - 1 - f
    NREAD = len(reads)

    places = [("turn", q) for q in range(NGRP)] + [("gram", kb) for kb in range(GBANKS)]

    mlp_products = ([(1, m, k) for m in range(M1) for k in range(KP + 1)]
                    + [(2, m, k) for m in range(M2) for k in range(M1)]
                    + [(3, 0, k) for k in range(M2)])
    MLP_GROUPS = M1 + M2 + 1
    SPLIT_AT = 3

    def mlp_at(tl, place):
        n, of = places.index(place) - SPLIT_AT - 1, len(places) - SPLIT_AT - 1
        total = len(mlp_products)
        return mlp_products[n * total // of:(n + 1) * total // of] if tl == TILES - 1 and n >= 0 else []

    def hot_at(tl, place, ahead=0):
        n, of = tl * len(places) + places.index(place), TILES * len(places)
        first = n * STEPS // of + ahead if n else 0
        return range(first, min((n + 1) * STEPS // of + ahead, STEPS))

    def slice_rows(k):
        return P if k == KD else min(P, NPAIR - k * P)

    def last_of_group(layer, k):
        return k == {1: KP, 2: M1 - 1, 3: M2 - 1}[layer]

    def group_index(layer, m):
        return m if layer == 1 else M1 + m if layer == 2 else M1 + M2

    with ExitStack() as ctx:
        def sb(name, shape, dt):
            return ctx.enter_context(nc.sbuf_tensor(name, shape, dt))

        def psum(name, shape):
            return ctx.enter_context(nc.psum_tensor(name, shape, F32))

        def sem(name):
            return ctx.enter_context(nc.semaphore(name))

        idx = sb("idx", [P, 4, len(tables)], I32)
        dense_in = sb("dense_in", [P, 4, D], F32)
        rows = sb("rows", [P, 2, NGATH, D], F32)
        turned = sb("turned", [P, 2, CHUNK, QUAD], F32)
        tab_hi = sb("tab_hi", [P, len(hot), CK, D], F32R)
        tab_lo = sb("tab_lo", [P, len(hot), CK, D], F32R)
        onehot = sb("onehot", [P, OH_BUFS, PAIRED, CHUNK], F32R)
        ids_f = sb("ids_f", [P, B], F16)
        pick = sb("pick", [P, len(hot), P], F16)
        row_no_i = sb("row_no_i", [P, CK], I32)
        row_no = sb("row_no", [P, CK], F32)
        ident = sb("ident", [P, P], F32)
        gram = sb("gram", [P, 2, FM, CHUNK // 4], F32)
        pairs = sb("pairs", [P, KP, CHUNK], F32)
        x_hi = sb("x_hi", [P, KP + 1, CHUNK], F32R)
        x_lo = sb("x_lo", [P, KP + 1, CHUNK], F32R)
        w1_hi = sb("w1_hi", [P, KP + 1, HID1], F32R)
        w1_lo = sb("w1_lo", [P, KP + 1, HID1], F32R)
        w2 = sb("w2", [P, M1, HID2], F32)
        w3 = sb("w3", [P, M2], F32)
        bias1 = sb("bias1", [P, M1], F32)
        bias2 = sb("bias2", [P, M2], F32)
        h1 = sb("h1", [P, M1, CHUNK], F32)
        h2 = sb("h2", [P, M2, CHUNK], F32)
        y = h1[0:1, 0, :]
        STAGES = 3
        stage = [gram[:].rearrange("p c g i -> p (c g i)")[0:VP, n * CK * D:(n + 1) * CK * D] for n in range(STAGES)]
        ids_in = turned[0:len(tables), 1, :, :].rearrange("p b f -> p (b f)")[:, 0:B].bitcast(I32)
        flat = [t[:].rearrange("p m n -> p (m n)") for t in (h1, h2, pairs)]
        w1_dense, w1_again = flat[0][:, 0:HID1], flat[0][:, HID1:2 * HID1]
        w1_in = [flat[1][:, 0:HID1], flat[2][:, 0:HID1], flat[0][:, HID1:2 * HID1]]
        assert KP == len(w1_in)

        ps_turn = [psum(f"ps_turn{n}", [P, 4, P]) for n in range(2)]
        ps_gram = [psum(f"ps_gram{n}", [P, 512]) for n in range(2)]
        ps_ids = psum("ps_ids", [P, PAIRED, CHUNK])
        ps_hot = psum("ps_hot", [P, PAIRED, CHUNK])
        ps_mlp = [psum(f"ps_mlp{n}", [P, 512]) for n in range(2)]

        idx_in = [sem(f"idx_in{n}") for n in range(4)]
        dense_up = [sem(f"dense_up{n}") for n in range(4)]
        gathers = [sem(f"gathers{n}") for n in range(4)]
        tiles_begun = sem("tiles_begun")
        ids_up = sem("ids_up")
        ids_ready = sem("ids_ready")
        stage_up = [sem(f"stage_up{n}") for n in range(STAGES)]
        hi_ready = sem("hi_ready")
        lo_ready = sem("lo_ready")
        w_up = sem("w_up")
        w1_dense_up = sem("w1_dense_up")
        w1_up = [sem(f"w1_up{k}") for k in range(KP)]
        w1_added = sem("w1_added")
        w1_hi_ready = sem("w1_hi_ready")
        w1_ready = sem("w1_ready")
        x_hi_ready = sem("x_hi_ready")
        x_ready = sem("x_ready")
        const_ready = sem("const_ready")
        row_no_ready = sem("row_no_ready")
        pads_ready = sem("pads_ready")
        turn_ready = sem("turn_ready")
        turn_out = sem("turn_out")
        ids_spread = sem("ids_spread")
        hot_ready = sem("hot_ready")
        hot_used = sem("hot_used")
        look_out = sem("look_out")
        gram_ready = sem("gram_ready")
        gram_out_a = sem("gram_out_a")
        gram_out_v = sem("gram_out_v")
        gram_stored = sem("gram_stored")
        pairs_up = sem("pairs_up")
        last_pairs_up = sem("last_pairs_up")
        mlp_ready = sem("mlp_ready")
        mlp_out = sem("mlp_out")
        y_stored = sem("y_stored")

        TURN0 = 2 * NGRP
        CONSTS = 4 + len(hot)
        MLP0 = MLP_GROUPS

        block_ = ctx.enter_context(nc.Block())

        def gram_src(kb, j):
            return ps_gram[kb % 2][j * QUAD:(j + 1) * QUAD, 0:GB * 4 * FM].rearrange(
                "f (i s g) -> f s i g", s=4, g=FM)[:, j, :, :]

        def gram_dst(par, tl, kb, j):
            at = tl * ROWS_QUAD + kb * GB
            return gram[j * QUAD:(j + 1) * QUAD, par, :, at:at + GB].rearrange("f g i -> f i g")

        full, rest = NPAIR // P, NPAIR % P

        def input_parts(to, par):
            parts = [(to[:, 0:full, :], pairs[:, 0:full, :])] if full else []
            if rest:
                parts.append((to[0:rest, full, :], pairs[0:rest, full, :]))
            parts.append((to[:, KD, :].rearrange("d (j l i) -> d j l i", j=4, l=TILES),
                          turned[:, par, :, 0].rearrange("d (l i j) -> d j l i", l=TILES, j=4)))
            return parts

        w1_slices = [(KD, w1_dense)] + list(enumerate(w1_in))

        LOOPS = (CHUNKS - 2) // 2
        EARLY_TURN = (UNITS // 2) * CK + CK // 2

        def both(p):
            return [(2 * p + 1, 1, p), (2 * p + 2, 0, p + 1)]

        last_reads = ([r for n, r in enumerate(reads) if n % 3 != 2], reads[2::3])

        def read_pairs(eng, c, read, done=pairs_up):
            f, g, n, k, row = read
            src = scratch[c].rearrange("(j f) g i -> f g j i", f=QUAD)[f, g - 1:g - 1 + n]
            dst = pairs[row:row + n, k, :].rearrange("r (j i) -> r j i", j=4)
            eng.dma_start(dst, src).then_inc(done, 16)

        @block_.sync
        def _(sp):
            def load_tile(row, tt):
                sp.dma_start(idx[:, tt, :], ids[bass.ds(row, P), :]).then_inc(idx_in[tt], 16)
                sp.dma_start(dense_in[:, tt, :], dense[bass.ds(row, P), :]).then_inc(dense_up[tt], 16)

            def chunk_step(c, par, nth, prefetch, shared=None):
                if prefetch:
                    for tl in range(TILES):
                        sp.wait_ge(turn_ready, TURN0 + NGRP * (TILES * c + tl + 1))
                        load_tile((c + 2) * CHUNK + tl * P, TILES * par + tl)
                sp.wait_ge(gram_out_a, TILES * GBANKS * (c + 1) + 2)
                sp.wait_ge(gram_out_v, TILES * GBANKS * (c + 1) + 2)
                sp.dma_start(scratch[c], gram[:, par, :, :]).then_inc(gram_stored, 16)
                if not (isinstance(c, int) and c == 0):
                    sp.wait_ge(x_ready, c)
                sp.wait_ge(gram_stored, 16 * (c + 1))
                for read in reads if shared is None else shared[0]:
                    read_pairs(sp, c, read)

            sp.dma_start(ids_in, ids_t).then_inc(ids_up, 16)
            load_tile(0, 0)
            for n, t in enumerate(hot):
                if n >= STAGES:
                    sp.wait_ge(lo_ready, n - STAGES + 1)
                sp.dma_start(stage[n % STAGES], tables[t].rearrange("(p c) d -> p (c d)", c=CK)).then_inc(
                    stage_up[n % STAGES], 16)
                if n < 3:
                    load_tile((n + 1) * P, n + 1)
            chunk_step(0, 0, 0, True)
            with sp.Fori(0, LOOPS - 1) as p:
                for c, par, nth in both(p):
                    chunk_step(c, par, nth, True)
            for c, par, nth in both(LOOPS - 1):
                chunk_step(c, par, nth, c + 2 < CHUNKS)
            chunk_step(CHUNKS - 1, 1, CHUNKS // 2 - 1, False, last_reads)
            sp.wait_ge(y_stored, 16 * CHUNKS)

        @block_.gpsimd
        def _(pool):
            nc.gpsimd.memset(pick[:], 0.0).then_inc(const_ready, 1)
            nc.gpsimd.memset(ident[:], 0.0).then_inc(const_ready, 1)
            nc.gpsimd.iota(row_no_i[:], [[1, CK]], base=0, channel_multiplier=CK).then_inc(const_ready, 1)
            pool.wait_ge(const_ready, 3)
            for n, t in enumerate(hot):
                nc.gpsimd.affine_select(out=pick[:, n, :], in_=pick[:, n, :], compare_op=ALU.not_equal, fill=1.0,
                                        base=-t, pattern=[[0, P]], channel_multiplier=1).then_inc(const_ready, 1)
            nc.gpsimd.affine_select(out=ident[:], in_=ident[:], compare_op=ALU.not_equal, fill=1.0, base=0,
                                    pattern=[[-1, P]], channel_multiplier=1).then_inc(const_ready, 1)
            with pool.Fori(0, CHUNKS // 2) as p:
                for tt in range(4):
                    pool.wait_ge(idx_in[tt], 16 * (p + 1))
                    pool.wait_ge(turn_ready, NGRP * (4 * p + tt + 1))
                    pool.sem_inc(tiles_begun, 1)
                    for n, t in enumerate(gathered):
                        pool.indirect_dma_start(
                            rows[:, tt % 2, n, :], None, tables[t],
                            bass.IndirectOffsetOnAxis(ap=idx[:, tt, t:t + 1], axis=0)).then_inc(gathers[tt], 16)
            pool.wait_ge(gram_stored, 16 * CHUNKS)
            pool.wait_ge(x_ready, CHUNKS - 1)
            for read in last_reads[1]:
                read_pairs(pool, CHUNKS - 1, read, last_pairs_up)

        @block_.tensor
        def _(pe):
            def spread_ids(chunk, u):
                if u or not (isinstance(chunk, int) and chunk == 0):
                    pe.wait_ge(hot_ready, chunk * STEPS + u * CK)
                for n in range(len(units[u])):
                    last = nc.tensor.matmul(ps_ids[:, n, :], pick[:, u * PAIRED + n, :],
                                            ids_f[:, bass.ds(chunk * CHUNK, CHUNK)], start=True, stop=True)
                last.then_inc(ids_spread, 1)

            def hot_step(chunk, s, tables_new=False):
                u, step = divmod(s, CK)
                if s == 0:
                    spread_ids(chunk, 0)
                if step == 0:
                    if tables_new:
                        pe.wait_ge(lo_ready, u * PAIRED + len(units[u]))
                    pe.wait_ge(look_out, chunk * UNITS + u + 1)
                pe.wait_ge(hot_ready, chunk * STEPS + s + 1)
                for n in range(len(units[u])):
                    for part, tab in enumerate((tab_hi, tab_lo)):
                        last = nc.tensor.matmul(ps_hot[:, n, :], tab[0:VP, u * PAIRED + n, step, :],
                                                onehot[0:VP, s % OH_BUFS, n, :],
                                                start=(step == 0 and part == 0 and n == 0),
                                                stop=(step == CK - 1 and part == 1), skip_group_check=True)
                last.then_inc(hot_used, 1)
                if step == CK - 2 and u + 1 < UNITS:
                    spread_ids(chunk, u + 1)

            def mlp_product(c, layer, m, k):
                g = group_index(layer, m)
                ps = ps_mlp[g % 2][:, 0:CHUNK]
                if k == 0:
                    pe.wait_ge(mlp_out, MLP_GROUPS * c + max(g, 1))
                if layer == 1:
                    if m == 0 and k == 0:
                        pe.wait_ge(x_ready, c + 1)
                    r = slice_rows(k)
                    for n, (w, x) in enumerate(((w1_hi, x_hi), (w1_hi, x_lo), (w1_lo, x_hi))):
                        last = nc.tensor.matmul(ps, w[0:r, k, m * P:(m + 1) * P], x[0:r, k, :],
                                                start=k == 0 and n == 0, stop=k == KP and n == 2)
                elif layer == 2:
                    pe.wait_ge(mlp_out, MLP_GROUPS * c + k + 2)
                    last = nc.tensor.matmul(ps, w2[:, k, m * P:(m + 1) * P], h1[:, k, :],
                                            start=k == 0, stop=k == M1 - 1)
                else:
                    pe.wait_ge(mlp_out, MLP_GROUPS * c + M1 + k + 2)
                    last = nc.tensor.matmul(ps[0:1, :], w3[:, k:k + 1], h2[:, k, :],
                                            start=k == 0, stop=k == M2 - 1)
                if last_of_group(layer, k):
                    last.then_inc(mlp_ready, 1)

            def turn_tile(c, par, nth, tl, mlp, hot_next):
                tt = TILES * par + tl
                pe.wait_ge(dense_up[tt], 16 * (nth + 1))
                pe.wait_ge(gathers[tt], 16 * NGATH * (nth + 1))
                for q, group in enumerate(groups):
                    pe.wait_ge(turn_out, NGRP * (TILES * c + tl) + q + 1)
                    for n, f in enumerate(group):
                        src = rows[:, tl, slot_of[f], :] if f else dense_in[:, tt, :]
                        last = nc.tensor.transpose(ps_turn[(NGRP * tt + q) % 2][:, n, :], src, ident[:])
                    last.then_inc(turn_ready, 1)
                    beside(c, tl, ("turn", q), mlp, hot_next)

            def mlp_whole(c):
                for product in mlp_products:
                    mlp_product(c, *product)

            def multiply_tile(c, par, tl, mlp, hot_next):
                pe.wait_ge(turn_out, NGRP * (TILES * c + tl + 1) + 2)
                pe.wait_ge(look_out, UNITS * (c + 1) + 1)
                for kb in range(GBANKS):
                    gram_bank(par, tl, kb, GBANKS * (TILES * c + tl) + kb)
                    beside(c, tl, ("gram", kb), mlp, hot_next)

            def beside(c, tl, place, mlp, hot_next):
                if hot_next:
                    for s in hot_at(tl, place):
                        hot_step(c + 1, s)
                if mlp:
                    for product in mlp_at(tl, place):
                        mlp_product(c - 1, *product)

            def chunk_step(c, par, nth, mlp=True, hot_next=True):
                for tl in range(TILES):
                    turn_tile(c, par, nth, tl, mlp, hot_next)
                    multiply_tile(c, par, tl, mlp, hot_next)

            def gram_bank(par, tl, kb, before):
                pe.wait_ge(gram_out_a, before + 1)
                pe.wait_ge(gram_out_v, before + 1)
                for i in range(GB):
                    at = tl * P + 4 * (kb * GB + i)
                    four = turned[:, par, at:at + 4, :]
                    last = nc.tensor.matmul(ps_gram[kb % 2][:, i * 4 * FM:(i + 1) * 4 * FM],
                                            four.rearrange("d b f -> d (b f)"), four[:, :, 1:F],
                                            start=True, stop=True)
                last.then_inc(gram_ready, 1)

            pe.sem_inc(turn_ready, TURN0)
            pe.sem_inc(mlp_ready, MLP0)
            pe.sem_inc(hot_used, OH_BUFS)
            pe.wait_ge(const_ready, CONSTS)
            pe.wait_ge(ids_ready, 1)
            for s in range(STEPS):
                hot_step(0, s, tables_new=True)
                if s == EARLY_TURN:
                    turn_tile(0, 0, 0, 0, False, False)
            pe.wait_ge(pads_ready, 3)
            for q in range(NGRP):
                beside(0, 0, ("turn", q), False, True)
            multiply_tile(0, 0, 0, False, True)
            turn_tile(0, 0, 0, 1, False, True)
            multiply_tile(0, 0, 1, False, True)
            pe.wait_ge(w1_ready, KP + 1)
            pe.wait_ge(w_up, 16 * 4)
            with pe.Fori(0, LOOPS) as p:
                for c, par, nth in both(p):
                    chunk_step(c, par, nth)
            c, par, nth = CHUNKS - 1, 1, CHUNKS // 2 - 1
            turn_tile(c, par, nth, 0, False, False)
            multiply_tile(c, par, 0, False, False)
            mlp_whole(c - 1)
            turn_tile(c, par, nth, 1, False, False)
            multiply_tile(c, par, 1, False, False)
            mlp_whole(c)

        @block_.scalar
        def _(act):
            def take_turned(c, par, tl, q):
                group = groups[q]
                ps = ps_turn[(NGRP * (TILES * par + tl) + q) % 2]
                act.wait_ge(turn_ready, TURN0 + NGRP * (TILES * c + tl) + q + 1)
                dst = turned[:, par, tl * P:(tl + 1) * P, stepped(group)].rearrange("d b f -> d f b")
                nc.scalar.activation(dst, ps[:, 0:len(group), :], ACT.Copy).then_inc(turn_out, 1)

            def take_lookups(c, par, u):
                act.wait_ge(hot_used, OH_BUFS + c * STEPS + (u + 1) * CK)
                for n, t in enumerate(units[u]):
                    last = nc.scalar.activation(turned[:, par, :, t + 1], ps_hot[:, n, :], ACT.Copy)
                last.then_inc(look_out, 1)

            def take_gram(c, par, nth, tl, kb):
                act.wait_ge(gram_ready, GBANKS * (TILES * c + tl) + kb + 1)
                if tl == 0 and kb == 0 and not (isinstance(nth, int) and nth == 0):
                    act.wait_ge(gram_stored, 16 * (c - 1))
                for j in ACT_QUADS:
                    last = nc.scalar.activation(gram_dst(par, tl, kb, j), gram_src(kb, j), ACT.Copy)
                last.then_inc(gram_out_a, 1)

            def take_mlp(c, layer, m, k):
                if not last_of_group(layer, k):
                    return
                g = group_index(layer, m)
                ps = ps_mlp[g % 2][:, 0:CHUNK]
                act.wait_ge(mlp_ready, MLP0 + MLP_GROUPS * c + g + 1)
                if layer == 1:
                    if m == 0 and not (isinstance(c, int) and c == 0):
                        act.wait_ge(y_stored, 16 * c)
                    nc.scalar.activation(h1[:, m, :], ps[:], ACT.Relu, bias=bias1[:, m:m + 1]).then_inc(mlp_out, 1)
                elif layer == 2:
                    nc.scalar.activation(h2[:, m, :], ps[:], ACT.Relu, bias=bias2[:, m:m + 1]).then_inc(mlp_out, 1)
                else:
                    nc.scalar.activation(y.rearrange("o (l i j) -> o j l i", j=4, l=TILES),
                                         ps[0:1, :].rearrange("o (j l i) -> o j l i", j=4, l=TILES),
                                         ACT.Copy).then_inc(mlp_out, 1)
                    act.wait_ge(mlp_out, MLP_GROUPS * (c + 1) + 1)
                    act.dma_start(out[bass.ds(c * CHUNK, CHUNK), :].rearrange("b o -> o b"), y).then_inc(y_stored, 16)

            def split_input(c, par):
                if isinstance(c, int) and c == CHUNKS - 1:
                    act.wait_ge(pairs_up, 16 * (NREAD * c + len(last_reads[0])))
                    act.wait_ge(last_pairs_up, 16 * len(last_reads[1]))
                else:
                    act.wait_ge(pairs_up, 16 * NREAD * (c + 1))
                for to, of in input_parts(x_hi, par):
                    last = nc.scalar.activation(to, of, ACT.Copy)
                last.then_inc(x_hi_ready, 1)

            def mlp_whole(c, par):
                split_input(c, par)
                for product in mlp_products:
                    take_mlp(c, *product)

            def turn_tile(c, par, tl, mlp, hot_next):
                for q in range(NGRP):
                    take_turned(c, par, tl, q)
                    if mlp and tl == TILES - 1 and q == SPLIT_AT:
                        split_input(c - 1, 1 - par)
                    beside(c, par, tl, ("turn", q), mlp, hot_next)

            def multiply_tile(c, par, nth, tl, mlp, hot_next):
                for kb in range(GBANKS):
                    take_gram(c, par, nth, tl, kb)
                    beside(c, par, tl, ("gram", kb), mlp, hot_next)

            def beside(c, par, tl, place, mlp, hot_next):
                if hot_next:
                    for s in hot_at(tl, place):
                        if s % CK == CK - 1:
                            take_lookups(c + 1, 1 - par, s // CK)
                if mlp:
                    for product in mlp_at(tl, place):
                        take_mlp(c - 1, *product)

            def chunk_step(c, par, nth, mlp=True, hot_next=True):
                for tl in range(TILES):
                    turn_tile(c, par, tl, mlp, hot_next)
                    multiply_tile(c, par, nth, tl, mlp, hot_next)

            act.sem_inc(turn_out, 2)
            act.sem_inc(look_out, 1)
            act.sem_inc(mlp_out, 1)
            act.sem_inc(gram_out_a, 2)
            act.dma_start(w1_dense, W1[0:D, :]).then_inc(w1_dense_up, 16)
            act.dma_start(w1_again, W1[D + NPAIR:, :]).then_inc(w1_dense_up, 16)

            def load_w1(k):
                n = slice_rows(k)
                act.dma_start(w1_in[k][0:n, :], W1[D + k * P:D + k * P + n, :]).then_inc(w1_up[k], 16)

            for k in range(KP - 1):
                load_w1(k)
            act.dma_start(w2[:], W2.rearrange("(k p) n -> p k n", p=P)).then_inc(w_up, 16)
            with nc.allow_non_contiguous_dma(reason="a few columns of biases and of the last layer"):
                act.dma_start(w3[:], W3.rearrange("(k p) o -> p (k o)", p=P)).then_inc(w_up, 16)
                act.dma_start(bias1[:], b1.rearrange("(m p) -> p m", p=P)).then_inc(w_up, 16)
                act.dma_start(bias2[:], b2.rearrange("(m p) -> p m", p=P)).then_inc(w_up, 16)
            for s in range(STEPS):
                for n, t in enumerate(hot):
                    if s == max(n // PAIRED - 1, 0) * CK:
                        act.wait_ge(stage_up[n % STAGES], 16 * (n // STAGES + 1))
                        nc.scalar.activation(tab_hi[0:VP, n, :, :],
                                             stage[n % STAGES].rearrange("p (c d) -> p c d", c=CK),
                                             ACT.Copy).then_inc(hi_ready, 1)
                if s % CK == CK - 1:
                    take_lookups(0, 0, s // CK)
                if s == EARLY_TURN:
                    turn_tile(0, 0, 0, False, False)
            for q in range(NGRP):
                beside(0, 0, 0, ("turn", q), False, True)
            multiply_tile(0, 0, 0, 0, False, True)
            act.wait_ge(w1_added, 1)
            load_w1(KP - 1)
            for k, of in w1_slices:
                if k != KD:
                    act.wait_ge(w1_up[k], 16)
                rows_k = slice_rows(k)
                nc.scalar.activation(w1_hi[0:rows_k, k, :], of[0:rows_k, :], ACT.Copy).then_inc(w1_hi_ready, 1)
            turn_tile(0, 0, 1, False, True)
            multiply_tile(0, 0, 0, 1, False, True)
            with act.Fori(0, LOOPS) as p:
                for c, par, nth in both(p):
                    chunk_step(c, par, nth)
            c, par, nth = CHUNKS - 1, 1, CHUNKS // 2 - 1
            turn_tile(c, par, 0, False, False)
            multiply_tile(c, par, nth, 0, False, False)
            mlp_whole(c - 1, 1 - par)
            turn_tile(c, par, 1, False, False)
            multiply_tile(c, par, nth, 1, False, False)
            mlp_whole(c, par)

        @block_.vector
        def _(dve):
            def make_hot(chunk, s):
                u, step = divmod(s, CK)
                if step == 0:
                    dve.wait_ge(ids_spread, chunk * UNITS + u + 1)
                dve.wait_ge(hot_used, chunk * STEPS + s + 1)
                w = len(units[u])
                nc.vector.tensor_scalar(onehot[0:VP, s % OH_BUFS, 0:w, :], ps_ids[0:VP, 0:w, :],
                                        row_no[0:VP, step:step + 1], None, ALU.is_equal).then_inc(hot_ready, 1)

            def take_gram(c, par, nth, tl, kb):
                dve.wait_ge(gram_ready, GBANKS * (TILES * c + tl) + kb + 1)
                if tl == 0 and kb == 0 and not (isinstance(nth, int) and nth == 0):
                    dve.wait_ge(gram_stored, 16 * (c - 1))
                for j in DVE_QUADS:
                    last = nc.vector.tensor_copy(gram_dst(par, tl, kb, j), gram_src(kb, j))
                last.then_inc(gram_out_v, 1)

            def split_input(c, par):
                dve.wait_ge(x_hi_ready, c + 1)
                for (to, of), (hi, _) in zip(input_parts(x_lo, par), input_parts(x_hi[:].bitcast(F32), par)):
                    last = nc.vector.tensor_tensor(to, of, hi, ALU.subtract)
                last.then_inc(x_ready, 1)

            def multiply_tile(c, par, nth, tl, mlp=False, hot_next=True):
                for place in places:
                    if mlp and tl == TILES - 1 and place == ("turn", SPLIT_AT):
                        split_input(c - 1, 1 - par)
                    if hot_next:
                        for s in hot_at(tl, place, HOT_AHEAD):
                            make_hot(c + 1, s)
                    if place[0] == "gram":
                        take_gram(c, par, nth, tl, place[1])

            dve.sem_inc(gram_out_v, 2)
            nc.vector.memset(ids_f[:].bitcast(F32), 0.0).then_inc(pads_ready, 1)
            dve.wait_ge(pads_ready, 1)
            dve.wait_ge(ids_up, 16)
            nc.vector.tensor_scalar(ids_f[0:len(tables), :], ids_in, 2047.0, None, ALU.min).then_inc(ids_ready, 1)
            dve.wait_ge(ids_ready, 1)
            for par in range(2):
                nc.vector.memset(turned[:, par, :, F:QUAD], 0.0).then_inc(pads_ready, 1)
            dve.wait_ge(const_ready, CONSTS)
            nc.vector.tensor_copy(row_no[:], row_no_i[:]).then_inc(row_no_ready, 1)
            dve.wait_ge(row_no_ready, 1)

            def low_part(n):
                dve.wait_ge(hi_ready, n + 1)
                nc.vector.tensor_tensor(tab_lo[0:VP, n, :, :], stage[n % STAGES].rearrange("p (c d) -> p c d", c=CK),
                                        tab_hi[0:VP, n, :, :].bitcast(F32), ALU.subtract).then_inc(lo_ready, 1)

            for s in range(STEPS):
                if s % CK == 0:
                    for n in range(len(units[s // CK])):
                        low_part(s // CK * PAIRED + n)
                make_hot(0, s)
            multiply_tile(0, 0, 0, 0)
            dve.wait_ge(w1_dense_up, 32)
            nc.vector.tensor_tensor(w1_dense, w1_dense, w1_again, ALU.add).then_inc(w1_added, 1)
            for n, (k, of) in enumerate(w1_slices):
                dve.wait_ge(w1_hi_ready, n + 1)
                rows_k = slice_rows(k)
                nc.vector.tensor_tensor(w1_lo[0:rows_k, k, :], of[0:rows_k, :], w1_hi[0:rows_k, k, :].bitcast(F32),
                                        ALU.subtract).then_inc(w1_ready, 1)
            multiply_tile(0, 0, 0, 1)
            with dve.Fori(0, LOOPS) as p:
                for c, par, nth in both(p):
                    for tl in range(TILES):
                        multiply_tile(c, par, nth, tl, mlp=True)
            c, par, nth = CHUNKS - 1, 1, CHUNKS // 2 - 1
            multiply_tile(c, par, nth, 0, hot_next=False)
            split_input(c - 1, 1 - par)
            multiply_tile(c, par, nth, 1, hot_next=False)
            split_input(c, par)


_TABLES = [f"tbl_{n}" for n in range(26)]
_INS = ["r_dense_output", "ids", "W_top1", "b_top1", "W_top2", "b_top2", "W_top3"] + _TABLES


def kernel(**inputs):
    import numpy as _np
    import concourse.bacc as _bacc
    from concourse import mybir as _mybir
    from concourse.bass_utils import run_bass_kernel_spmd as _run

    nc = _bacc.Bacc("TRN2", target_bir_lowering=False, num_devices=1)
    arrays, aps = {}, {}
    given = {name: inputs[name] for name in _INS}
    given["ids_t"] = _np.asarray(inputs["ids"]).T
    for name, value in given.items():
        a = _np.ascontiguousarray(value)
        arrays[f"in_{name}"] = a
        aps[name] = nc.dram_tensor(f"in_{name}", a.shape, _mybir.dt.from_np(a.dtype), kind="ExternalInput").ap()
    rows, dt = aps["ids"].shape[0], _mybir.dt.float32
    out = nc.dram_tensor("out", (rows, 1), dt, kind="ExternalOutput").ap()
    features = len(_TABLES) + 1
    scratch = nc.dram_tensor("gram_scratch", (rows // CHUNK, P, features - 1, CHUNK // 4), dt, kind="Internal").ap()
    build(nc, aps["r_dense_output"], aps["ids"], aps["ids_t"], [aps[t] for t in _TABLES], aps["W_top1"],
          aps["b_top1"], aps["W_top2"], aps["b_top2"], aps["W_top3"], scratch, out)
    r = _run(nc, [arrays], core_ids=[0])
    return r.results[0]["out"]
```

```python
from contextlib import ExitStack

import concourse.bass as bass
from concourse import mybir

F32 = mybir.dt.float32
F32R = mybir.dt.float32r
F16 = mybir.dt.float16
I32 = mybir.dt.int32
ALU = mybir.AluOpType
ACT = mybir.ActivationFunctionType

P = 128
CHUNK = 256
TILES = CHUNK // P
QUAD = 32
ROWS_QUAD = P // 4
PAIRED = 2
OH_BUFS = 4
SPREAD_AT = 4
HOT_AHEAD = 2
HOT_TABLES = 6


def uniform_groups(features, most):
    groups = []
    for f in features:
        g = groups[-1] if groups else None
        if g and len(g) < most and (len(g) == 1 or f - g[-1] == g[-1] - g[-2]):
            g.append(f)
        else:
            groups.append([f])
    return groups


def stepped(group):
    step = group[1] - group[0] if len(group) > 1 else 1
    return slice(group[0], group[-1] + 1, step)


def pair_lines(sparse, rows):
    long = [(d, 0, sparse) for d in range(1, sparse // 2)]
    short = [(sparse // 2, 0, sparse // 2), (0, 0, sparse)]
    lines, room = [], rows
    while long or short:
        if long and long[0][2] <= room:
            d, s, n = long.pop(0)
        else:
            d, s, n = short.pop(0)
            if n > room:
                short.insert(0, (d, s + room, n - room))
                n = room
        lines.append((d, s, n))
        room = room - n or rows
    return lines


def pair_list(sparse, rows):
    return [tuple(sorted((m + 1 if d else 0, (m + d) % sparse + 1)))
            for d, s, n in pair_lines(sparse, rows) for m in range(s, s + n)]


def build(nc, dense, ids, ids_t, tables, W1, b1, W2, b2, W3, scratch, out):
    B, D = dense.shape
    F = len(tables) + 1
    HID1, HID2 = W2.shape
    NPAIR = F * (F - 1) // 2
    CHUNKS = B // CHUNK
    KP = -(-NPAIR // P)
    KR = -(-NPAIR // KP)
    KD = KP
    M1, M2 = HID1 // P, HID2 // P
    assert D == P and W1.shape[0] == D + NPAIR + D and F <= QUAD

    hot = sorted(sorted(range(len(tables)), key=lambda t: tables[t].shape[0])[:HOT_TABLES])
    VOCAB = tables[hot[0]].shape[0]
    CK = -(-VOCAB // P)
    VP = VOCAB // CK
    assert all(tables[t].shape[0] == VP * CK for t in hot) and VOCAB <= 2048
    gathered = [t for t in range(len(tables)) if t not in hot]
    NGATH = len(gathered)
    slot_of = {t + 1: n for n, t in enumerate(gathered)}
    groups = uniform_groups([0] + [t + 1 for t in gathered], 4)
    NGRP = len(groups)
    units = [hot[n:n + PAIRED] for n in range(0, len(hot), PAIRED)]
    UNITS = len(units)
    STEPS = UNITS * CK
    GB = 4
    GBANKS = ROWS_QUAD // GB
    FM = F - 1
    ACT_QUADS, DVE_QUADS = (0, 1), (2, 3)

    WIDE = FM + FM // 2 - 1
    assert FM % 2 == 0 and KP * KR == NPAIR and scratch.shape[2] == QUAD * WIDE
    reads, at = [], 0
    for d, first, n in pair_lines(FM, KR):
        cell, step = ((first + 1) * WIDE + first + d, WIDE + 1) if d else (first, 1)
        reads.append((cell, step, n, at // KR, at % KR))
        at += n
    NREAD = len(reads)

    places = [("turn", q) for q in range(NGRP)] + [("gram", kb) for kb in range(GBANKS)]

    chunk_places = [(tl, place) for tl in range(TILES) for place in places]

    mlp_products = ([(1, m, k) for m in range(M1) for k in range(KP + 1)]
                    + [(2, m, k) for m in range(M2) for k in range(M1)]
                    + [(3, 0, k) for k in range(M2)])
    MLP_GROUPS = M1 + M2 + 1
    SPLIT_AFTER = (0, ("gram", GBANKS - 1))
    MLP_AFTER = (1, ("turn", 1))

    def mlp_at(tl, place):
        n = chunk_places.index((tl, place)) - chunk_places.index(MLP_AFTER) - 1
        of = len(chunk_places) - chunk_places.index(MLP_AFTER) - 1
        total = len(mlp_products)
        return mlp_products[n * total // of:(n + 1) * total // of] if n >= 0 else []

    gram_places, before_place = TILES * GBANKS, [0]
    spread_steps = STEPS - (TILES * NGRP - 1)
    for tl, (kind, n) in chunk_places:
        if kind == "turn":
            here = int((tl, n) != (0, 0))
        else:
            g = tl * GBANKS + n
            here = (g + 1) * spread_steps // gram_places - g * spread_steps // gram_places
        before_place.append(before_place[-1] + here)

    def hot_at(tl, place, ahead=0):
        n = chunk_places.index((tl, place))
        first = before_place[n] + ahead if n else 0
        return range(min(first, STEPS), min(before_place[n + 1] + ahead, STEPS))

    def slice_rows(k):
        return P if k == KD else KR

    def last_of_group(layer, k):
        return k == {1: KP, 2: M1 - 1, 3: M2 - 1}[layer]

    def group_index(layer, m):
        return m if layer == 1 else M1 + m if layer == 2 else M1 + M2

    with ExitStack() as ctx:
        def sb(name, shape, dt):
            return ctx.enter_context(nc.sbuf_tensor(name, shape, dt))

        def psum(name, shape):
            return ctx.enter_context(nc.psum_tensor(name, shape, F32))

        def sem(name):
            return ctx.enter_context(nc.semaphore(name))

        idx = sb("idx", [P, 4, len(tables)], I32)
        dense_in = sb("dense_in", [P, 4, D], F32)
        rows = sb("rows", [P, 2, NGATH, D], F32)
        turned = sb("turned", [P, 2, CHUNK, QUAD], F32)
        tab_hi = sb("tab_hi", [P, len(hot), CK, D], F32R)
        tab_lo = sb("tab_lo", [P, len(hot), CK, D], F32R)
        onehot = sb("onehot", [P, OH_BUFS, PAIRED, CHUNK], F32R)
        ids_f = sb("ids_f", [P, B], F16)
        pick = sb("pick", [P, len(hot), P], F16)
        ids_all = sb("ids_all", [P, 2, PAIRED, CHUNK], F32)
        row_no_i = sb("row_no_i", [P, CK], I32)
        row_no = sb("row_no", [P, CK], F32)
        ident = sb("ident", [P, P], F32)
        gram = sb("gram", [P, 2, FM, CHUNK // 4], F32)
        pairs = sb("pairs", [P, KP, CHUNK], F32)
        x_hi = sb("x_hi", [P, KP + 1, CHUNK], F32R)
        x_lo = sb("x_lo", [P, KP + 1, CHUNK], F32R)
        w1_hi = sb("w1_hi", [P, KP + 1, HID1], F32R)
        w1_lo = sb("w1_lo", [P, KP + 1, HID1], F32R)
        w2 = sb("w2", [P, M1, HID2], F32)
        w3 = sb("w3", [P, M2], F32)
        bias1 = sb("bias1", [P, M1], F32)
        bias2 = sb("bias2", [P, M2], F32)
        h1 = sb("h1", [P, M1, CHUNK], F32)
        h2 = sb("h2", [P, M2, CHUNK], F32)
        y = h1[0:1, 0, :]
        STAGES = 3
        stage = [gram[:].rearrange("p c g i -> p (c g i)")[0:VP, n * CK * D:(n + 1) * CK * D] for n in range(STAGES)]
        ids_in = turned[0:len(tables), 1, :, :].rearrange("p b f -> p (b f)")[:, 0:B].bitcast(I32)
        flat = [t[:].rearrange("p m n -> p (m n)") for t in (h1, h2, pairs)]
        w1_dense, w1_again = flat[0][:, 0:HID1], flat[0][:, HID1:2 * HID1]
        w1_in = [flat[1][:, 0:HID1], flat[2][:, 0:HID1], flat[0][:, HID1:2 * HID1]]
        assert KP == len(w1_in)

        ps_turn = [psum(f"ps_turn{n}", [P, 4, P]) for n in range(2)]
        ps_gram = [psum(f"ps_gram{n}", [P, 512]) for n in range(2)]
        ps_ids = psum("ps_ids", [P, PAIRED, CHUNK])
        ps_hot = psum("ps_hot", [P, PAIRED, CHUNK])
        ps_mlp = [psum(f"ps_mlp{n}", [P, 512]) for n in range(2)]

        idx_in = [sem(f"idx_in{n}") for n in range(4)]
        dense_up = [sem(f"dense_up{n}") for n in range(4)]
        gathers = [sem(f"gathers{n}") for n in range(4)]
        tiles_begun = sem("tiles_begun")
        ids_up = sem("ids_up")
        ids_ready = sem("ids_ready")
        stage_up = [sem(f"stage_up{n}") for n in range(STAGES)]
        hi_ready = sem("hi_ready")
        lo_ready = sem("lo_ready")
        w_up = sem("w_up")
        w1_dense_up = sem("w1_dense_up")
        w1_up = [sem(f"w1_up{k}") for k in range(KP)]
        w1_added = sem("w1_added")
        w1_hi_ready = sem("w1_hi_ready")
        w1_ready = sem("w1_ready")
        x_hi_ready = sem("x_hi_ready")
        x_ready = sem("x_ready")
        const_ready = sem("const_ready")
        row_no_ready = sem("row_no_ready")
        pads_ready = sem("pads_ready")
        turn_ready = sem("turn_ready")
        turn_out = sem("turn_out")
        ids_spread = sem("ids_spread")
        ids_out = sem("ids_out")
        hot_ready = sem("hot_ready")
        hot_used = sem("hot_used")
        look_out = sem("look_out")
        gram_ready = sem("gram_ready")
        gram_out_a = sem("gram_out_a")
        gram_out_v = sem("gram_out_v")
        gram_stored = sem("gram_stored")
        again_stored = sem("again_stored")
        pairs_up = sem("pairs_up")
        last_pairs_up = sem("last_pairs_up")
        mlp_ready = sem("mlp_ready")
        mlp_out = sem("mlp_out")
        y_stored = sem("y_stored")

        TURN0 = 2 * NGRP
        CONSTS = 4 + len(hot)
        MLP0 = MLP_GROUPS

        block_ = ctx.enter_context(nc.Block())

        def ids_buffer(par, u):
            return ids_all[:, (UNITS * par + u) % 2, 0:len(units[u]), :]

        def gram_src(kb, j):
            return ps_gram[kb % 2][j * QUAD:(j + 1) * QUAD, 0:GB * 4 * FM].rearrange(
                "f (i s g) -> f s i g", s=4, g=FM)[:, j, :, :]

        def gram_dst(par, tl, kb, j):
            at = tl * ROWS_QUAD + kb * GB
            return gram[j * QUAD:(j + 1) * QUAD, par, :, at:at + GB].rearrange("f g i -> f i g")

        def input_parts(to, par):
            parts = [(to[0:KR, 0:KP, :], pairs[0:KR, :, :])]
            parts.append((to[:, KD, :].rearrange("d (j l i) -> d j l i", j=4, l=TILES),
                          turned[:, par, :, 0].rearrange("d (l i j) -> d j l i", l=TILES, j=4)))
            return parts

        w1_slices = [(KD, w1_dense)] + list(enumerate(w1_in))

        LOOPS = (CHUNKS - 2) // 2

        def both(p):
            return [(2 * p + 1, 1, p), (2 * p + 2, 0, p + 1)]

        last_reads = ([r for n, r in enumerate(reads) if n % 3 != 2], reads[2::3])

        def store_gram(c, par):
            to = scratch[c].rearrange("j (f g) i -> (j f) g i", g=WIDE)
            nc.sync.dma_start(to[:, 0:FM, :], gram[:, par, :, :]).then_inc(gram_stored, 16)
            nc.sync.dma_start(to[:, FM:WIDE, :], gram[:, par, 0:WIDE - FM, :]).then_inc(again_stored, 16)

        def read_pairs(eng, c, read, done=pairs_up):
            cell, step, n, k, row = read
            src = scratch[c][:, cell:cell + (n - 1) * step + 1:step, :].rearrange("j g i -> g j i")
            dst = pairs[row:row + n, k, :].rearrange("r (j i) -> r j i", j=4)
            eng.dma_start(dst, src).then_inc(done, 16)

        @block_.sync
        def _(sp):
            def load_tile(row, tt):
                sp.dma_start(idx[:, tt, :], ids[bass.ds(row, P), :]).then_inc(idx_in[tt], 16)
                sp.dma_start(dense_in[:, tt, :], dense[bass.ds(row, P), :]).then_inc(dense_up[tt], 16)

            def chunk_step(c, par, nth, prefetch, shared=None):
                if prefetch:
                    for tl in range(TILES):
                        sp.wait_ge(turn_ready, TURN0 + NGRP * (TILES * c + tl + 1))
                        load_tile((c + 2) * CHUNK + tl * P, TILES * par + tl)
                sp.wait_ge(gram_out_a, TILES * GBANKS * (c + 1) + 2)
                sp.wait_ge(gram_out_v, TILES * GBANKS * (c + 1) + 2)
                store_gram(c, par)
                if not (isinstance(c, int) and c == 0):
                    sp.wait_ge(x_ready, c)
                sp.wait_ge(gram_stored, 16 * (c + 1))
                sp.wait_ge(again_stored, 16 * (c + 1))
                for read in reads if shared is None else shared[0]:
                    read_pairs(sp, c, read)

            sp.dma_start(ids_in, ids_t).then_inc(ids_up, 16)
            for n, t in enumerate(hot):
                if n >= STAGES:
                    sp.wait_ge(lo_ready, n - STAGES + 1)
                sp.dma_start(stage[n % STAGES], tables[t].rearrange("(p c) d -> p (c d)", c=CK)).then_inc(
                    stage_up[n % STAGES], 16)
                if n < 4:
                    load_tile(n * P, n)
            chunk_step(0, 0, 0, True)
            with sp.Fori(0, LOOPS - 1) as p:
                for c, par, nth in both(p):
                    chunk_step(c, par, nth, True)
            for c, par, nth in both(LOOPS - 1):
                chunk_step(c, par, nth, c + 2 < CHUNKS)
            chunk_step(CHUNKS - 1, 1, CHUNKS // 2 - 1, False, last_reads)
            sp.wait_ge(y_stored, 16 * CHUNKS)

        @block_.gpsimd
        def _(pool):
            nc.gpsimd.memset(pick[:], 0.0).then_inc(const_ready, 1)
            nc.gpsimd.memset(ident[:], 0.0).then_inc(const_ready, 1)
            nc.gpsimd.iota(row_no_i[:], [[1, CK]], base=0, channel_multiplier=CK).then_inc(const_ready, 1)
            pool.wait_ge(const_ready, 3)
            for n, t in enumerate(hot):
                nc.gpsimd.affine_select(out=pick[:, n, :], in_=pick[:, n, :], compare_op=ALU.not_equal, fill=1.0,
                                        base=-t, pattern=[[0, P]], channel_multiplier=1).then_inc(const_ready, 1)
            nc.gpsimd.affine_select(out=ident[:], in_=ident[:], compare_op=ALU.not_equal, fill=1.0, base=0,
                                    pattern=[[-1, P]], channel_multiplier=1).then_inc(const_ready, 1)
            with pool.Fori(0, CHUNKS // 2) as p:
                for tt in range(4):
                    pool.wait_ge(idx_in[tt], 16 * (p + 1))
                    pool.wait_ge(turn_ready, NGRP * (4 * p + tt + 1))
                    pool.sem_inc(tiles_begun, 1)
                    for n, t in enumerate(gathered):
                        pool.indirect_dma_start(
                            rows[:, tt % 2, n, :], None, tables[t],
                            bass.IndirectOffsetOnAxis(ap=idx[:, tt, t:t + 1], axis=0)).then_inc(gathers[tt], 16)
            pool.wait_ge(gram_stored, 16 * CHUNKS)
            pool.wait_ge(again_stored, 16 * CHUNKS)
            pool.wait_ge(x_ready, CHUNKS - 1)
            for read in last_reads[1]:
                read_pairs(pool, CHUNKS - 1, read, last_pairs_up)

        @block_.tensor
        def _(pe):
            def spread_ids(chunk, u):
                if u or not (isinstance(chunk, int) and chunk == 0):
                    pe.wait_ge(ids_out, chunk * UNITS + u)
                for n in range(len(units[u])):
                    last = nc.tensor.matmul(ps_ids[:, n, :], pick[:, u * PAIRED + n, :],
                                            ids_f[:, bass.ds(chunk * CHUNK, CHUNK)], start=True, stop=True)
                last.then_inc(ids_spread, 1)

            def hot_step(chunk, s, tables_new=False):
                u, step = divmod(s, CK)
                if step == 0:
                    if tables_new:
                        pe.wait_ge(lo_ready, u * PAIRED + len(units[u]))
                    pe.wait_ge(look_out, chunk * UNITS + u + 1)
                pe.wait_ge(hot_ready, chunk * STEPS + s + 1)
                for n in range(len(units[u])):
                    for part, tab in enumerate((tab_hi, tab_lo)):
                        last = nc.tensor.matmul(ps_hot[:, n, :], tab[0:VP, u * PAIRED + n, step, :],
                                                onehot[0:VP, s % OH_BUFS, n, :],
                                                start=(step == 0 and part == 0 and n == 0),
                                                stop=(step == CK - 1 and part == 1), skip_group_check=True)
                last.then_inc(hot_used, 1)
                if step == SPREAD_AT and u + 1 < UNITS:
                    spread_ids(chunk, u + 1)

            def mlp_product(c, layer, m, k):
                g = group_index(layer, m)
                ps = ps_mlp[g % 2][:, 0:CHUNK]
                if k == 0:
                    pe.wait_ge(mlp_out, MLP_GROUPS * c + max(g, 1))
                if layer == 1:
                    if m == 0 and k == 0:
                        pe.wait_ge(x_ready, c + 1)
                    r = slice_rows(k)
                    for n, (w, x) in enumerate(((w1_hi, x_hi), (w1_hi, x_lo), (w1_lo, x_hi))):
                        last = nc.tensor.matmul(ps, w[0:r, k, m * P:(m + 1) * P], x[0:r, k, :],
                                                start=k == 0 and n == 0, stop=k == KP and n == 2)
                elif layer == 2:
                    pe.wait_ge(mlp_out, MLP_GROUPS * c + k + 2)
                    last = nc.tensor.matmul(ps, w2[:, k, m * P:(m + 1) * P], h1[:, k, :],
                                            start=k == 0, stop=k == M1 - 1)
                else:
                    pe.wait_ge(mlp_out, MLP_GROUPS * c + M1 + k + 2)
                    last = nc.tensor.matmul(ps[0:1, :], w3[:, k:k + 1], h2[:, k, :],
                                            start=k == 0, stop=k == M2 - 1)
                if last_of_group(layer, k):
                    last.then_inc(mlp_ready, 1)

            def turn_tile(c, par, nth, tl, mlp, hot_next):
                if hot_next and tl == 0:
                    spread_ids(c + 1, 0)
                tt = TILES * par + tl
                pe.wait_ge(dense_up[tt], 16 * (nth + 1))
                pe.wait_ge(gathers[tt], 16 * NGATH * (nth + 1))
                for q, group in enumerate(groups):
                    pe.wait_ge(turn_out, NGRP * (TILES * c + tl) + q + 1)
                    for n, f in enumerate(group):
                        src = rows[:, tl, slot_of[f], :] if f else dense_in[:, tt, :]
                        last = nc.tensor.transpose(ps_turn[(NGRP * tt + q) % 2][:, n, :], src, ident[:])
                    last.then_inc(turn_ready, 1)
                    beside(c, tl, ("turn", q), mlp, hot_next)

            def mlp_whole(c):
                for product in mlp_products:
                    mlp_product(c, *product)

            def multiply_tile(c, par, tl, mlp, hot_next):
                pe.wait_ge(turn_out, NGRP * (TILES * c + tl + 1) + 2)
                pe.wait_ge(look_out, UNITS * (c + 1) + 1)
                for kb in range(GBANKS):
                    gram_bank(par, tl, kb, GBANKS * (TILES * c + tl) + kb)
                    beside(c, tl, ("gram", kb), mlp, hot_next)

            def beside(c, tl, place, mlp, hot_next):
                if hot_next:
                    for s in hot_at(tl, place):
                        hot_step(c + 1, s)
                if mlp:
                    for product in mlp_at(tl, place):
                        mlp_product(c - 1, *product)

            def chunk_step(c, par, nth, mlp=True, hot_next=True):
                for tl in range(TILES):
                    turn_tile(c, par, nth, tl, mlp, hot_next)
                    multiply_tile(c, par, tl, mlp, hot_next)

            def gram_bank(par, tl, kb, before):
                pe.wait_ge(gram_out_a, before + 1)
                pe.wait_ge(gram_out_v, before + 1)
                for i in range(GB):
                    at = tl * P + 4 * (kb * GB + i)
                    four = turned[:, par, at:at + 4, :]
                    last = nc.tensor.matmul(ps_gram[kb % 2][:, i * 4 * FM:(i + 1) * 4 * FM],
                                            four.rearrange("d b f -> d (b f)"), four[:, :, 1:F],
                                            start=True, stop=True)
                last.then_inc(gram_ready, 1)

            pe.sem_inc(turn_ready, TURN0)
            pe.sem_inc(mlp_ready, MLP0)
            pe.sem_inc(hot_used, OH_BUFS)
            pe.wait_ge(const_ready, CONSTS)
            pe.wait_ge(ids_ready, 1)
            spread_ids(0, 0)
            for s in range(STEPS):
                hot_step(0, s, tables_new=True)
            pe.wait_ge(pads_ready, 3)
            chunk_step(0, 0, 0, mlp=False)
            pe.wait_ge(w1_ready, KP + 1)
            pe.wait_ge(w_up, 16 * 4)
            with pe.Fori(0, LOOPS) as p:
                for c, par, nth in both(p):
                    chunk_step(c, par, nth)
            c, par, nth = CHUNKS - 1, 1, CHUNKS // 2 - 1
            turn_tile(c, par, nth, 0, False, False)
            multiply_tile(c, par, 0, False, False)
            turn_tile(c, par, nth, 1, False, False)
            multiply_tile(c, par, 1, False, False)
            mlp_whole(c - 1)
            mlp_whole(c)

        @block_.scalar
        def _(act):
            def take_turned(c, par, tl, q):
                group = groups[q]
                ps = ps_turn[(NGRP * (TILES * par + tl) + q) % 2]
                act.wait_ge(turn_ready, TURN0 + NGRP * (TILES * c + tl) + q + 1)
                dst = turned[:, par, tl * P:(tl + 1) * P, stepped(group)].rearrange("d b f -> d f b")
                nc.scalar.activation(dst, ps[:, 0:len(group), :], ACT.Copy).then_inc(turn_out, 1)

            def take_ids(chunk, par, u):
                act.wait_ge(ids_spread, chunk * UNITS + u + 1)
                if u > 1 or not (isinstance(chunk, int) and chunk == 0):
                    act.wait_ge(hot_ready, chunk * STEPS + (u - 1) * CK)
                nc.scalar.activation(ids_buffer(par, u), ps_ids[:, 0:len(units[u]), :], ACT.Copy).then_inc(ids_out, 1)

            def take_lookups(c, par, u):
                act.wait_ge(hot_used, OH_BUFS + c * STEPS + (u + 1) * CK)
                for n, t in enumerate(units[u]):
                    last = nc.scalar.activation(turned[:, par, :, t + 1], ps_hot[:, n, :], ACT.Copy)
                last.then_inc(look_out, 1)

            def hot_step(chunk, par, s):
                u, step = divmod(s, CK)
                if step == SPREAD_AT and u + 1 < UNITS:
                    take_ids(chunk, par, u + 1)
                if step == CK - 1:
                    take_lookups(chunk, par, u)

            def take_gram(c, par, nth, tl, kb):
                act.wait_ge(gram_ready, GBANKS * (TILES * c + tl) + kb + 1)
                if tl == 0 and kb == 0 and not (isinstance(nth, int) and nth == 0):
                    act.wait_ge(gram_stored, 16 * (c - 1))
                    act.wait_ge(again_stored, 16 * (c - 1))
                for j in ACT_QUADS:
                    last = nc.scalar.activation(gram_dst(par, tl, kb, j), gram_src(kb, j), ACT.Copy)
                last.then_inc(gram_out_a, 1)

            def take_mlp(c, layer, m, k):
                if not last_of_group(layer, k):
                    return
                g = group_index(layer, m)
                ps = ps_mlp[g % 2][:, 0:CHUNK]
                act.wait_ge(mlp_ready, MLP0 + MLP_GROUPS * c + g + 1)
                if layer == 1:
                    if m == 0 and not (isinstance(c, int) and c == 0):
                        act.wait_ge(y_stored, 16 * c)
                    nc.scalar.activation(h1[:, m, :], ps[:], ACT.Relu, bias=bias1[:, m:m + 1]).then_inc(mlp_out, 1)
                elif layer == 2:
                    nc.scalar.activation(h2[:, m, :], ps[:], ACT.Relu, bias=bias2[:, m:m + 1]).then_inc(mlp_out, 1)
                else:
                    nc.scalar.activation(y.rearrange("o (l i j) -> o j l i", j=4, l=TILES),
                                         ps[0:1, :].rearrange("o (j l i) -> o j l i", j=4, l=TILES),
                                         ACT.Copy).then_inc(mlp_out, 1)
                    act.wait_ge(mlp_out, MLP_GROUPS * (c + 1) + 1)
                    act.dma_start(out[bass.ds(c * CHUNK, CHUNK), :].rearrange("b o -> o b"), y).then_inc(y_stored, 16)

            def split_input(c, par):
                if isinstance(c, int) and c == CHUNKS - 1:
                    act.wait_ge(pairs_up, 16 * (NREAD * c + len(last_reads[0])))
                    act.wait_ge(last_pairs_up, 16 * len(last_reads[1]))
                else:
                    act.wait_ge(pairs_up, 16 * NREAD * (c + 1))
                for to, of in input_parts(x_hi, par):
                    last = nc.scalar.activation(to, of, ACT.Copy)
                last.then_inc(x_hi_ready, 1)

            def mlp_whole(c):
                for product in mlp_products:
                    take_mlp(c, *product)

            def turn_tile(c, par, tl, mlp, hot_next):
                if hot_next and tl == 0:
                    take_ids(c + 1, 1 - par, 0)
                for q in range(NGRP):
                    take_turned(c, par, tl, q)
                    beside(c, par, tl, ("turn", q), mlp, hot_next)

            def multiply_tile(c, par, nth, tl, mlp, hot_next):
                for kb in range(GBANKS):
                    take_gram(c, par, nth, tl, kb)
                    beside(c, par, tl, ("gram", kb), mlp, hot_next)

            def beside(c, par, tl, place, mlp, hot_next):
                if mlp and (tl, place) == SPLIT_AFTER:
                    split_input(c - 1, 1 - par)
                if hot_next:
                    for s in hot_at(tl, place):
                        hot_step(c + 1, 1 - par, s)
                if mlp:
                    for product in mlp_at(tl, place):
                        take_mlp(c - 1, *product)

            def chunk_step(c, par, nth, mlp=True, hot_next=True):
                for tl in range(TILES):
                    turn_tile(c, par, tl, mlp, hot_next)
                    multiply_tile(c, par, nth, tl, mlp, hot_next)

            act.sem_inc(turn_out, 2)
            act.sem_inc(look_out, 1)
            act.sem_inc(mlp_out, 1)
            act.sem_inc(gram_out_a, 2)

            def load_w1(k):
                n = slice_rows(k)
                act.dma_start(w1_in[k][0:n, :], W1[D + k * KR:D + k * KR + n, :]).then_inc(w1_up[k], 16)

            def load_weights():
                act.dma_start(w1_dense, W1[0:D, :]).then_inc(w1_dense_up, 16)
                act.dma_start(w1_again, W1[D + NPAIR:, :]).then_inc(w1_dense_up, 16)
                for k in range(KP - 1):
                    load_w1(k)
                act.dma_start(w2[:], W2.rearrange("(k p) n -> p k n", p=P)).then_inc(w_up, 16)
                with nc.allow_non_contiguous_dma(reason="a few columns of biases and of the last layer"):
                    act.dma_start(w3[:], W3.rearrange("(k p) o -> p (k o)", p=P)).then_inc(w_up, 16)
                    act.dma_start(bias1[:], b1.rearrange("(m p) -> p m", p=P)).then_inc(w_up, 16)
                    act.dma_start(bias2[:], b2.rearrange("(m p) -> p m", p=P)).then_inc(w_up, 16)

            take_ids(0, 0, 0)
            for s in range(STEPS):
                for n, t in enumerate(hot):
                    if s == max(n // PAIRED - 1, 0) * CK:
                        act.wait_ge(stage_up[n % STAGES], 16 * (n // STAGES + 1))
                        nc.scalar.activation(tab_hi[0:VP, n, :, :],
                                             stage[n % STAGES].rearrange("p (c d) -> p c d", c=CK),
                                             ACT.Copy).then_inc(hi_ready, 1)
                if s == CK - 1:
                    load_weights()
                hot_step(0, 0, s)
            turn_tile(0, 0, 0, False, True)
            multiply_tile(0, 0, 0, 0, False, True)
            act.wait_ge(w1_added, 1)
            load_w1(KP - 1)
            for k, of in w1_slices:
                if k != KD:
                    act.wait_ge(w1_up[k], 16)
                rows_k = slice_rows(k)
                nc.scalar.activation(w1_hi[0:rows_k, k, :], of[0:rows_k, :], ACT.Copy).then_inc(w1_hi_ready, 1)
            turn_tile(0, 0, 1, False, True)
            multiply_tile(0, 0, 0, 1, False, True)
            with act.Fori(0, LOOPS) as p:
                for c, par, nth in both(p):
                    chunk_step(c, par, nth)
            c, par, nth = CHUNKS - 1, 1, CHUNKS // 2 - 1
            turn_tile(c, par, 0, False, False)
            multiply_tile(c, par, nth, 0, False, False)
            split_input(c - 1, 1 - par)
            turn_tile(c, par, 1, False, False)
            multiply_tile(c, par, nth, 1, False, False)
            mlp_whole(c - 1)
            split_input(c, par)
            mlp_whole(c)

        @block_.vector
        def _(dve):
            def make_hot(chunk, par, s):
                u, step = divmod(s, CK)
                if step == 0:
                    dve.wait_ge(ids_out, chunk * UNITS + u + 1)
                dve.wait_ge(hot_used, chunk * STEPS + s + 1)
                w = len(units[u])
                nc.vector.tensor_scalar(onehot[0:VP, s % OH_BUFS, 0:w, :], ids_buffer(par, u)[0:VP],
                                        row_no[0:VP, step:step + 1], None, ALU.is_equal).then_inc(hot_ready, 1)

            def take_gram(c, par, nth, tl, kb):
                dve.wait_ge(gram_ready, GBANKS * (TILES * c + tl) + kb + 1)
                if tl == 0 and kb == 0 and not (isinstance(nth, int) and nth == 0):
                    dve.wait_ge(gram_stored, 16 * (c - 1))
                    dve.wait_ge(again_stored, 16 * (c - 1))
                for j in DVE_QUADS:
                    last = nc.vector.tensor_copy(gram_dst(par, tl, kb, j), gram_src(kb, j))
                last.then_inc(gram_out_v, 1)

            def split_input(c, par):
                dve.wait_ge(x_hi_ready, c + 1)
                for (to, of), (hi, _) in zip(input_parts(x_lo, par), input_parts(x_hi[:].bitcast(F32), par)):
                    last = nc.vector.tensor_tensor(to, of, hi, ALU.subtract)
                last.then_inc(x_ready, 1)

            def multiply_tile(c, par, nth, tl, mlp=False, hot_next=True):
                for place in places:
                    if hot_next:
                        for s in hot_at(tl, place, HOT_AHEAD):
                            make_hot(c + 1, 1 - par, s)
                    if place[0] == "gram":
                        take_gram(c, par, nth, tl, place[1])
                    if mlp and (tl, place) == SPLIT_AFTER:
                        split_input(c - 1, 1 - par)

            dve.sem_inc(gram_out_v, 2)
            nc.vector.memset(ids_f[:].bitcast(F32), 0.0).then_inc(pads_ready, 1)
            dve.wait_ge(pads_ready, 1)
            dve.wait_ge(ids_up, 16)
            nc.vector.tensor_scalar(ids_f[0:len(tables), :], ids_in, 2047.0, None, ALU.min).then_inc(ids_ready, 1)
            dve.wait_ge(ids_ready, 1)
            for par in range(2):
                nc.vector.memset(turned[:, par, :, F:QUAD], 0.0).then_inc(pads_ready, 1)
            dve.wait_ge(const_ready, CONSTS)
            nc.vector.tensor_copy(row_no[:], row_no_i[:]).then_inc(row_no_ready, 1)
            dve.wait_ge(row_no_ready, 1)

            def low_part(n):
                dve.wait_ge(hi_ready, n + 1)
                nc.vector.tensor_tensor(tab_lo[0:VP, n, :, :], stage[n % STAGES].rearrange("p (c d) -> p c d", c=CK),
                                        tab_hi[0:VP, n, :, :].bitcast(F32), ALU.subtract).then_inc(lo_ready, 1)

            for s in range(STEPS):
                if s % CK == 0:
                    for n in range(len(units[s // CK])):
                        low_part(s // CK * PAIRED + n)
                make_hot(0, 0, s)
            multiply_tile(0, 0, 0, 0)
            dve.wait_ge(w1_dense_up, 32)
            nc.vector.tensor_tensor(w1_dense, w1_dense, w1_again, ALU.add).then_inc(w1_added, 1)
            for n, (k, of) in enumerate(w1_slices):
                dve.wait_ge(w1_hi_ready, n + 1)
                rows_k = slice_rows(k)
                nc.vector.tensor_tensor(w1_lo[0:rows_k, k, :], of[0:rows_k, :], w1_hi[0:rows_k, k, :].bitcast(F32),
                                        ALU.subtract).then_inc(w1_ready, 1)
            multiply_tile(0, 0, 0, 1)
            with dve.Fori(0, LOOPS) as p:
                for c, par, nth in both(p):
                    for tl in range(TILES):
                        multiply_tile(c, par, nth, tl, mlp=True)
            c, par, nth = CHUNKS - 1, 1, CHUNKS // 2 - 1
            multiply_tile(c, par, nth, 0, hot_next=False)
            split_input(c - 1, 1 - par)
            multiply_tile(c, par, nth, 1, hot_next=False)
            split_input(c, par)


_TABLES = [f"tbl_{n}" for n in range(26)]
_INS = ["r_dense_output", "ids", "W_top1", "b_top1", "W_top2", "b_top2", "W_top3"] + _TABLES


def kernel(**inputs):
    import numpy as _np
    import concourse.bacc as _bacc
    from concourse import mybir as _mybir
    from concourse.bass_utils import run_bass_kernel_spmd as _run

    nc = _bacc.Bacc("TRN2", target_bir_lowering=False, num_devices=1)
    arrays, aps = {}, {}
    given = {name: inputs[name] for name in _INS}
    given["ids_t"] = _np.asarray(inputs["ids"]).T
    w1, dim, sparse = _np.asarray(inputs["W_top1"]), inputs["r_dense_output"].shape[1], len(_TABLES)
    number = {pair: n for n, pair in enumerate((f, g) for f in range(sparse + 1) for g in range(f + 1, sparse + 1))}
    order = [number[pair] for pair in pair_list(sparse, len(number) // -(-len(number) // P))]
    given["W_top1"] = _np.concatenate([w1[:dim], w1[dim:-dim][order], w1[-dim:]])
    for name, value in given.items():
        a = _np.ascontiguousarray(value)
        arrays[f"in_{name}"] = a
        aps[name] = nc.dram_tensor(f"in_{name}", a.shape, _mybir.dt.from_np(a.dtype), kind="ExternalInput").ap()
    rows, dt = aps["ids"].shape[0], _mybir.dt.float32
    out = nc.dram_tensor("out", (rows, 1), dt, kind="ExternalOutput").ap()
    scratch = nc.dram_tensor("gram_scratch", (rows // CHUNK, 4, QUAD * (len(_TABLES) * 3 // 2 - 1), CHUNK // 4), dt, kind="Internal").ap()
    build(nc, aps["r_dense_output"], aps["ids"], aps["ids_t"], [aps[t] for t in _TABLES], aps["W_top1"],
          aps["b_top1"], aps["W_top2"], aps["b_top2"], aps["W_top3"], scratch, out)
    r = _run(nc, [arrays], core_ids=[0])
    return r.results[0]["out"]
```

```python
from contextlib import ExitStack

import concourse.bass as bass
from concourse import mybir

F32 = mybir.dt.float32
F32R = mybir.dt.float32r
F16 = mybir.dt.float16
I32 = mybir.dt.int32
ALU = mybir.AluOpType
ACT = mybir.ActivationFunctionType

P = 128
CHUNK = 256
TILES = CHUNK // P
QUAD = 32
ROWS_QUAD = P // 4
PAIRED = 2
OH_BUFS = 4
SPREAD_AT = 3
HOT_AHEAD = 3
HOT_TABLES = 7
ODD_ONLY = 1


def uniform_groups(features, most):
    groups = []
    for f in features:
        g = groups[-1] if groups else None
        if g and len(g) < most and (len(g) == 1 or f - g[-1] == g[-1] - g[-2]):
            g.append(f)
        else:
            groups.append([f])
    return groups


def stepped(group):
    step = group[1] - group[0] if len(group) > 1 else 1
    return slice(group[0], group[-1] + 1, step)


def pair_lines(sparse, rows):
    long = [(d, 0, sparse) for d in range(1, sparse // 2)]
    short = [(sparse // 2, 0, sparse // 2), (0, 0, sparse)]
    lines, room = [], rows
    while long or short:
        if long and long[0][2] <= room:
            d, s, n = long.pop(0)
        else:
            d, s, n = short.pop(0)
            if n > room:
                short.insert(0, (d, s + room, n - room))
                n = room
        lines.append((d, s, n))
        room = room - n or rows
    return lines


def pair_list(sparse, rows):
    return [tuple(sorted((m + 1 if d else 0, (m + d) % sparse + 1)))
            for d, s, n in pair_lines(sparse, rows) for m in range(s, s + n)]


def build(nc, dense, ids, ids_t, tables, W1, b1, W2, b2, W3, scratch, out):
    B, D = dense.shape
    F = len(tables) + 1
    HID1, HID2 = W2.shape
    NPAIR = F * (F - 1) // 2
    CHUNKS = B // CHUNK
    KP = -(-NPAIR // P)
    KR = -(-NPAIR // KP)
    KD = KP
    M1, M2 = HID1 // P, HID2 // P
    assert D == P and W1.shape[0] == D + NPAIR + D and F <= QUAD

    hot = sorted(sorted(range(len(tables)), key=lambda t: tables[t].shape[0])[:HOT_TABLES])
    VOCAB = tables[hot[0]].shape[0]
    CK = -(-VOCAB // P)
    VP = VOCAB // CK
    assert all(tables[t].shape[0] == VP * CK for t in hot) and VOCAB <= 2048
    hot_of = [hot[:len(hot) - ODD_ONLY], hot]
    gathered = [[t for t in range(len(tables)) if t not in hot_of[par]] for par in range(2)]
    slot_of = [{t + 1: n for n, t in enumerate(gathered[par])} for par in range(2)]
    groups = [uniform_groups([0] + [t + 1 for t in gathered[par]], 4) for par in range(2)]
    NGRP = len(groups[0])
    assert len(groups[1]) == NGRP
    group_of = [{f: q for q, group in enumerate(groups[par]) for f in group} for par in range(2)]
    units = [[hot_of[par][n:n + PAIRED] for n in range(0, len(hot_of[par]), PAIRED)] for par in range(2)]
    UNITS = [len(units[par]) for par in range(2)]
    STEPS = [UNITS[par] * CK for par in range(2)]
    assert max(UNITS) <= 4 and all(steps % OH_BUFS == 0 for steps in STEPS)
    GB = 4
    GBANKS = ROWS_QUAD // GB
    FM = F - 1
    ACT_QUADS, DVE_QUADS = (0, 1), (2, 3)

    WIDE = FM + FM // 2 - 1
    assert FM % 2 == 0 and KP * KR == NPAIR and scratch.shape[2] == QUAD * WIDE
    reads, at = [], 0
    for d, first, n in pair_lines(FM, KR):
        cell, step = ((first + 1) * WIDE + first + d, WIDE + 1) if d else (first, 1)
        reads.append((cell, step, n, at // KR, at % KR))
        at += n
    NREAD = len(reads)

    places = [("turn", q) for q in range(NGRP)] + [("gram", kb) for kb in range(GBANKS)]
    chunk_places = [(tl, place) for tl in range(TILES) for place in places]

    slices = [KD] + list(range(KP))
    mlp_products = ([(1, m, k) for m in range(M1) for k in slices]
                    + [(2, m, k) for m in range(M2) for k in range(M1)]
                    + [(3, 0, k) for k in range(M2)])
    MLP_GROUPS = M1 + M2 + 1
    SPLIT_AFTER = (0, ("gram", GBANKS - 1))
    MLP_AFTER = (1, ("turn", 1))

    def mlp_at(tl, place):
        n = chunk_places.index((tl, place)) - chunk_places.index(MLP_AFTER) - 1
        of = len(chunk_places) - chunk_places.index(MLP_AFTER) - 1
        total = len(mlp_products)
        return mlp_products[n * total // of:(n + 1) * total // of] if n >= 0 else []

    assert NGRP <= GBANKS
    last_places = [(0, ("turn", q)) for q in range(NGRP)]
    for kb in range(GBANKS):
        last_places.append((0, ("gram", kb)))
        if kb < NGRP - 1 or kb == GBANKS - 1:
            last_places.append((1, ("turn", min(kb, NGRP - 1))))
    last_places += [(1, ("gram", kb)) for kb in range(GBANKS)]

    last_products = ([(1, m, k) for k in slices for m in range(M1)]
                     + [product for product in mlp_products if product[0] > 1])
    LAST_SPLIT_AFTER = (1, ("turn", NGRP - 1))

    before_place = []
    for par in range(2):
        counts, gram_places = [0], TILES * GBANKS
        spread_steps = STEPS[par] - (TILES * NGRP - 1)
        for tl, (kind, n) in chunk_places:
            if kind == "turn":
                here = int((tl, n) != (0, 0))
            else:
                g = tl * GBANKS + n
                here = (g + 1) * spread_steps // gram_places - g * spread_steps // gram_places
            counts.append(counts[-1] + here)
        before_place.append(counts)

    def hot_at(par, tl, place, ahead=0):
        n = chunk_places.index((tl, place))
        first = before_place[par][n] + ahead if n else 0
        return range(min(first, STEPS[par]), min(before_place[par][n + 1] + ahead, STEPS[par]))

    def slice_rows(k):
        return P if k == KD else KR

    def last_of_group(layer, k):
        return k == {1: KP - 1, 2: M1 - 1, 3: M2 - 1}[layer]

    def group_index(layer, m):
        return m if layer == 1 else M1 + m if layer == 2 else M1 + M2

    with ExitStack() as ctx:
        def sb(name, shape, dt):
            return ctx.enter_context(nc.sbuf_tensor(name, shape, dt))

        def psum(name, shape):
            return ctx.enter_context(nc.psum_tensor(name, shape, F32))

        def sem(name):
            return ctx.enter_context(nc.semaphore(name))

        idx = sb("idx", [P, 4, len(tables)], I32)
        dense_in = sb("dense_in", [P, TILES, D], F32)
        rows = sb("rows", [P, 2, len(gathered[0]), D], F32)
        turned = sb("turned", [P, 2, CHUNK, QUAD], F32)
        tab_hi = sb("tab_hi", [P, len(hot), CK, D], F32R)
        tab_lo = sb("tab_lo", [P, len(hot), CK, D], F32R)
        onehot = sb("onehot", [P, OH_BUFS, PAIRED, CHUNK], F32R)
        ids_f = sb("ids_f", [P, B + CHUNK], F16)
        pick = sb("pick", [P, len(hot), P], F16)
        ids_all = sb("ids_all", [P, 3, PAIRED, CHUNK], F16)
        row_no_i = sb("row_no_i", [P, CK], I32)
        row_no = sb("row_no", [P, CK], F32)
        ident = sb("ident", [P, P], F32)
        gram = sb("gram", [P, 2, FM, CHUNK // 4], F32)
        pairs = sb("pairs", [P, KP, CHUNK], F32)
        x_hi = sb("x_hi", [P, KP + 1, CHUNK], F32R)
        x_lo = sb("x_lo", [P, KP + 1, CHUNK], F32R)
        w1_hi = sb("w1_hi", [P, KP + 1, HID1], F32R)
        w1_lo = sb("w1_lo", [P, KP + 1, HID1], F32R)
        w2 = sb("w2", [P, M1, HID2], F32)
        w3 = sb("w3", [P, M2], F32)
        bias1 = sb("bias1", [P, M1], F32)
        bias2 = sb("bias2", [P, M2], F32)
        h1 = sb("h1", [P, M1, CHUNK], F32)
        y = h1[0:1, 0, :]
        STAGES = 3
        stage = [gram[:].rearrange("p c g i -> p (c g i)")[0:VP, n * CK * D:(n + 1) * CK * D] for n in range(STAGES)]
        ids_in = turned[0:len(tables), 1, :, :].rearrange("p b f -> p (b f)")[:, 0:B].bitcast(I32)
        flat = [t[:].rearrange("p m n -> p (m n)") for t in (h1, w2, pairs)]
        w1_dense, w1_again = flat[0][:, 0:HID1], flat[0][:, HID1:2 * HID1]
        w1_in = [flat[1][:, 0:HID1], flat[2][:, 0:HID1], flat[0][:, HID1:2 * HID1]]
        assert KP == len(w1_in)

        ps_turn = [psum(f"ps_turn{n}", [P, 4, P]) for n in range(2)]
        ps_gram = [psum(f"ps_gram{n}", [P, 512]) for n in range(2)]
        ps_ids = psum("ps_ids", [P, PAIRED, CHUNK])
        ps_hot = psum("ps_hot", [P, PAIRED, CHUNK])
        ps_mlp = [psum(f"ps_mlp{n}", [P, 512]) for n in range(2)]

        idx_in = [sem(f"idx_in{n}") for n in range(4)]
        dense_up = [sem(f"dense_up{n}") for n in range(TILES)]
        gathers = [[sem(f"gathers{n}_{q}") for q in range(NGRP)] for n in range(4)]
        tiles_begun = sem("tiles_begun")
        ids_up = sem("ids_up")
        ids_ready = sem("ids_ready")
        stage_up = [sem(f"stage_up{n}") for n in range(STAGES)]
        hi_ready = sem("hi_ready")
        lo_ready = sem("lo_ready")
        w_up = sem("w_up")
        w1_dense_up = sem("w1_dense_up")
        w1_up = [sem(f"w1_up{k}") for k in range(KP)]
        w1_added = sem("w1_added")
        w1_hi_ready = sem("w1_hi_ready")
        w1_ready = sem("w1_ready")
        x_hi_ready = sem("x_hi_ready")
        x_ready = sem("x_ready")
        const_ready = sem("const_ready")
        row_no_ready = sem("row_no_ready")
        pads_ready = sem("pads_ready")
        turn_ready = sem("turn_ready")
        turn_out = sem("turn_out")
        turn_out_v = sem("turn_out_v")
        ids_spread = sem("ids_spread")
        ids_out = sem("ids_out")
        hot_ready = sem("hot_ready")
        hot_used = sem("hot_used")
        look_out = sem("look_out")
        gram_ready = sem("gram_ready")
        gram_out_a = sem("gram_out_a")
        gram_out_v = sem("gram_out_v")
        gram_stored = sem("gram_stored")
        again_stored = sem("again_stored")
        pairs_up = sem("pairs_up")
        last_up = [[sem(f"last_up_{eng}{k}") for k in range(KP)] for eng in ("sp", "pool")]
        mlp_ready = sem("mlp_ready")
        mlp_out = sem("mlp_out")
        y_stored = sem("y_stored")

        TURN0 = 2 * NGRP
        CONSTS = 4 + len(hot)

        block_ = ctx.enter_context(nc.Block())

        def h2_of(c):
            if isinstance(c, int) and c >= CHUNKS - 2:
                return gram[:, 0, 0:M2 * 4, :].rearrange("p g i -> p (g i)").rearrange(
                    "p (m n) -> p m n", m=M2)
            return pairs[:, 0:M2, :]

        def is_first(c):
            return isinstance(c, int) and c == 0

        def is_last(c):
            return isinstance(c, int) and c == CHUNKS - 1

        def mlp_bank(c, layer, m):
            if is_last(c) and layer == 1 and m >= 2:
                return ps_turn[m % 2][:].rearrange("p f b -> p (f b)")[:, 0:CHUNK]
            return ps_mlp[group_index(layer, m) % 2][:, 0:CHUNK]

        def places_of(c):
            return last_places if is_last(c) else chunk_places

        def turned_by_dve(c, tl, q):
            return is_last(c) and (NGRP * tl + q) % 2 == 1

        def take_turned(copy_out, par, tl, q):
            group = groups[par][q]
            dst = turned[:, par, tl * P:(tl + 1) * P, stepped(group)].rearrange("d b f -> d f b")
            return copy_out(dst, ps_turn[(NGRP * (TILES * par + tl) + q) % 2][:, 0:len(group), :])

        def after(h):
            c, par, nth = h
            return c + 1, 1 - par, nth + par

        def units_before(h):
            _, par, nth = h
            return nth * sum(UNITS) + par * UNITS[0]

        def ids_buffer(par, u):
            return ids_all[:, u if u < 3 else 1, 0:len(units[par][u]), :]

        def gram_src(kb, j):
            return ps_gram[kb % 2][j * QUAD:(j + 1) * QUAD, 0:GB * 4 * FM].rearrange(
                "f (i s g) -> f s i g", s=4, g=FM)[:, j, :, :]

        def gram_dst(par, tl, kb, j):
            at = tl * ROWS_QUAD + kb * GB
            return gram[j * QUAD:(j + 1) * QUAD, par, :, at:at + GB].rearrange("f g i -> f i g")

        def input_slice(to, par, k):
            if k != KD:
                return to[0:KR, k, :], pairs[0:KR, k, :]
            return (to[:, KD, :].rearrange("d (j l i) -> d j l i", j=4, l=TILES),
                    turned[:, par, :, 0].rearrange("d (l i j) -> d j l i", l=TILES, j=4))

        def input_parts(to, par):
            return [(to[0:KR, 0:KP, :], pairs[0:KR, :, :]), input_slice(to, par, KD)]

        w1_slices = [(KD, w1_dense)] + list(enumerate(w1_in))
        w1_add_after = (0, ("turn", NGRP - 1))
        w1_places = [(0, ("gram", 1 + n * (GBANKS - 1) // len(w1_slices))) for n in range(len(w1_slices))]

        LOOPS = (CHUNKS - 2) // 2

        def both(p):
            return [(2 * p + 1, 1, p), (2 * p + 2, 0, p + 1)]

        last_reads = ([r for n, r in enumerate(reads) if n % 3 != 2], reads[2::3])

        def store_gram(c, par):
            to = scratch[c].rearrange("j (f g) i -> (j f) g i", g=WIDE)
            nc.sync.dma_start(to[:, 0:FM, :], gram[:, par, :, :]).then_inc(gram_stored, 16)
            nc.sync.dma_start(to[:, FM:WIDE, :], gram[:, par, 0:WIDE - FM, :]).then_inc(again_stored, 16)

        def read_pairs(eng, c, read, done):
            cell, step, n, k, row = read
            src = scratch[c][:, cell:cell + (n - 1) * step + 1:step, :].rearrange("j g i -> g j i")
            dst = pairs[row:row + n, k, :].rearrange("r (j i) -> r j i", j=4)
            eng.dma_start(dst, src).then_inc(done, 16)

        @block_.sync
        def _(sp):
            def load_idx(row, tt):
                sp.dma_start(idx[:, tt, :], ids[bass.ds(row, P), :]).then_inc(idx_in[tt], 16)

            def load_dense(row, tl):
                sp.dma_start(dense_in[:, tl, :], dense[bass.ds(row, P), :]).then_inc(dense_up[tl], 16)

            def store_y(c):
                sp.wait_ge(mlp_out, MLP_GROUPS * (c + 1) + 1)
                sp.dma_start(out[bass.ds(c * CHUNK, CHUNK), :].rearrange("b o -> o b"), y).then_inc(y_stored, 16)

            def chunk_step(c, par, nth, prefetch, last=False):
                for tl in range(TILES if prefetch else 0):
                    sp.wait_ge(turn_ready, TURN0 + NGRP * (TILES * c + tl + 1))
                    load_dense((c + 1) * CHUNK + tl * P, tl)
                    if prefetch > 1:
                        load_idx((c + 2) * CHUNK + tl * P, TILES * par + tl)
                sp.wait_ge(gram_out_a, TILES * GBANKS * (c + 1) + 2)
                sp.wait_ge(gram_out_v, TILES * GBANKS * (c + 1) + 2)
                store_gram(c, par)
                if not is_first(c) and not is_last(c):
                    store_y(c - 1)
                if not is_first(c):
                    sp.wait_ge(x_ready, c)
                sp.wait_ge(gram_stored, 16 * (c + 1))
                sp.wait_ge(again_stored, 16 * (c + 1))
                for read in last_reads[0] if last else reads:
                    read_pairs(nc.sync, c, read, last_up[0][read[3]] if last else pairs_up)

            def load_w1(k):
                n = slice_rows(k)
                sp.dma_start(w1_in[k][0:n, :], W1[D + k * KR:D + k * KR + n, :]).then_inc(w1_up[k], 16)

            def load_weights():
                sp.dma_start(w1_dense, W1[0:D, :]).then_inc(w1_dense_up, 16)
                sp.dma_start(w1_again, W1[D + NPAIR:, :]).then_inc(w1_dense_up, 16)
                for k in range(KP - 1):
                    load_w1(k)
                with nc.allow_non_contiguous_dma(reason="a few columns of biases and of the last layer"):
                    sp.dma_start(w3[:], W3.rearrange("(k p) o -> p (k o)", p=P)).then_inc(w_up, 16)
                    sp.dma_start(bias1[:], b1.rearrange("(m p) -> p m", p=P)).then_inc(w_up, 16)
                    sp.dma_start(bias2[:], b2.rearrange("(m p) -> p m", p=P)).then_inc(w_up, 16)

            sp.dma_start(ids_in, ids_t).then_inc(ids_up, 16)
            for n, t in enumerate(hot):
                if n >= STAGES:
                    sp.wait_ge(lo_ready, n - STAGES + 1)
                sp.dma_start(stage[n % STAGES], tables[t].rearrange("(p c) d -> p (c d)", c=CK)).then_inc(
                    stage_up[n % STAGES], 16)
                if n < 4:
                    load_idx(n * P, n)
                if n < TILES:
                    load_dense(n * P, n)
            load_weights()
            sp.wait_ge(w1_added, 1)
            load_w1(KP - 1)
            sp.wait_ge(w1_ready, KP + 1)
            sp.dma_start(w2[:], W2.rearrange("(k p) n -> p k n", p=P)).then_inc(w_up, 16)
            chunk_step(0, 0, 0, 2)
            with sp.Fori(0, LOOPS - 1) as p:
                for c, par, nth in both(p):
                    chunk_step(c, par, nth, 2)
            for c, par, nth in both(LOOPS - 1):
                chunk_step(c, par, nth, min(CHUNKS - 1 - c, 2))
            chunk_step(CHUNKS - 1, 1, CHUNKS // 2 - 1, 0, last=True)
            store_y(CHUNKS - 2)
            store_y(CHUNKS - 1)
            sp.wait_ge(y_stored, 16 * CHUNKS)

        @block_.gpsimd
        def _(pool):
            nc.gpsimd.memset(pick[:], 0.0).then_inc(const_ready, 1)
            nc.gpsimd.memset(ident[:], 0.0).then_inc(const_ready, 1)
            nc.gpsimd.iota(row_no_i[:], [[1, CK]], base=0, channel_multiplier=CK).then_inc(const_ready, 1)
            pool.wait_ge(const_ready, 3)
            for n, t in enumerate(hot):
                nc.gpsimd.affine_select(out=pick[:, n, :], in_=pick[:, n, :], compare_op=ALU.not_equal, fill=1.0,
                                        base=-t, pattern=[[0, P]], channel_multiplier=1).then_inc(const_ready, 1)
            nc.gpsimd.affine_select(out=ident[:], in_=ident[:], compare_op=ALU.not_equal, fill=1.0, base=0,
                                    pattern=[[-1, P]], channel_multiplier=1).then_inc(const_ready, 1)
            with pool.Fori(0, CHUNKS // 2) as p:
                for tt in range(4):
                    pool.wait_ge(idx_in[tt], 16 * (p + 1))
                    pool.wait_ge(turn_ready, NGRP * (4 * p + tt + 1))
                    pool.sem_inc(tiles_begun, 1)
                    for n, t in enumerate(gathered[tt // TILES]):
                        pool.indirect_dma_start(
                            rows[:, tt % 2, n, :], None, tables[t],
                            bass.IndirectOffsetOnAxis(ap=idx[:, tt, t:t + 1], axis=0)).then_inc(
                                gathers[tt][group_of[tt // TILES][t + 1]], 16)
            pool.wait_ge(gram_stored, 16 * CHUNKS)
            pool.wait_ge(again_stored, 16 * CHUNKS)
            pool.wait_ge(x_ready, CHUNKS - 1)
            for read in last_reads[1]:
                read_pairs(pool, CHUNKS - 1, read, last_up[1][read[3]])

        @block_.tensor
        def _(pe):
            def spread_ids(h, u):
                if u or not is_first(h[0]):
                    pe.wait_ge(ids_out, units_before(h) + u)
                for n in range(len(units[h[1]][u])):
                    last = nc.tensor.matmul(ps_ids[:, n, :], pick[:, u * PAIRED + n, :],
                                            ids_f[:, bass.ds(h[0] * CHUNK, CHUNK)], start=True, stop=True)
                last.then_inc(ids_spread, 1)

            def hot_step(h, s, tables_new=False):
                par, (u, step) = h[1], divmod(s, CK)
                unit = units[par][u]
                if step == 0:
                    if tables_new:
                        pe.wait_ge(lo_ready, u * PAIRED + len(unit))
                    pe.wait_ge(look_out, units_before(h) + u + 1)
                pe.wait_ge(hot_ready, CK * units_before(h) + s + 1)
                for n in range(len(unit)):
                    for part, tab in enumerate((tab_hi, tab_lo)):
                        last = nc.tensor.matmul(ps_hot[:, n, :], tab[0:VP, u * PAIRED + n, step, :],
                                                onehot[0:VP, s % OH_BUFS, n, :],
                                                start=(step == 0 and part == 0 and n == 0),
                                                stop=(step == CK - 1 and part == 1), skip_group_check=True)
                last.then_inc(hot_used, 1)
                if step == SPREAD_AT:
                    if u + 1 < UNITS[par]:
                        spread_ids(h, u + 1)
                    else:
                        spread_ids(after(h), 0)

            def mlp_product(c, layer, m, k):
                g, ps = group_index(layer, m), mlp_bank(c, layer, m)
                if k == (KD if layer == 1 else 0) and not (is_last(c) and layer == 1 and m >= 2):
                    pe.wait_ge(mlp_out, MLP_GROUPS * c + max(g, 1))
                if layer == 1:
                    if is_last(c):
                        pe.wait_ge(x_ready, c + 1 + slices.index(k))
                    elif m == 0 and k == KD:
                        pe.wait_ge(x_ready, c + 1)
                    r = slice_rows(k)
                    for n, (w, x) in enumerate(((w1_hi, x_hi), (w1_hi, x_lo), (w1_lo, x_hi))):
                        last = nc.tensor.matmul(ps, w[0:r, k, m * P:(m + 1) * P], x[0:r, k, :],
                                                start=k == KD and n == 0, stop=k == KP - 1 and n == 2)
                elif layer == 2:
                    pe.wait_ge(mlp_out, MLP_GROUPS * c + k + 2)
                    last = nc.tensor.matmul(ps, w2[:, k, m * P:(m + 1) * P], h1[:, k, :],
                                            start=k == 0, stop=k == M1 - 1)
                else:
                    pe.wait_ge(mlp_out, MLP_GROUPS * c + M1 + k + 2)
                    last = nc.tensor.matmul(ps[0:1, :], w3[:, k:k + 1], h2_of(c)[:, k, :],
                                            start=k == 0, stop=k == M2 - 1)
                if last_of_group(layer, k):
                    last.then_inc(mlp_ready, 1)

            def turn_group(c, par, nth, tl, q):
                tt, group = TILES * par + tl, groups[par][q]
                if q == 0:
                    pe.wait_ge(dense_up[tl], 16 * (c + 1))
                pe.wait_ge(gathers[tt][q], 16 * sum(f > 0 for f in group) * (nth + 1))
                here = NGRP * tl + q
                if not is_last(c) or here < 2:
                    pe.wait_ge(turn_out, NGRP * TILES * c + here + 1)
                elif here % 2:
                    pe.wait_ge(turn_out_v, here // 2)
                else:
                    pe.wait_ge(turn_out, NGRP * TILES * c + here // 2 + 2)
                for n, f in enumerate(group):
                    src = rows[:, tl, slot_of[par][f], :] if f else dense_in[:, tl, :]
                    last = nc.tensor.transpose(ps_turn[(NGRP * tt + q) % 2][:, n, :], src, ident[:])
                last.then_inc(turn_ready, 1)

            def multiply_bank(c, par, nth, tl, kb):
                if kb == 0:
                    here = NGRP * (tl + 1)
                    if is_last(c):
                        pe.wait_ge(turn_out, NGRP * TILES * c + -(-here // 2) + 2)
                        pe.wait_ge(turn_out_v, here // 2)
                    else:
                        pe.wait_ge(turn_out, NGRP * TILES * c + here + 2)
                    pe.wait_ge(look_out, units_before(after((c, par, nth))) + 1)
                gram_bank(par, tl, kb, GBANKS * (TILES * c + tl) + kb)

            def chunk_step(c, par, nth, mlp=True, hot_next=True):
                for tl, (kind, n) in places_of(c):
                    (turn_group if kind == "turn" else multiply_bank)(c, par, nth, tl, n)
                    if hot_next:
                        for s in hot_at(1 - par, tl, (kind, n)):
                            hot_step(after((c, par, nth)), s)
                    if mlp:
                        for product in mlp_at(tl, (kind, n)):
                            mlp_product(c - 1, *product)

            def gram_bank(par, tl, kb, before):
                pe.wait_ge(gram_out_a, before + 1)
                pe.wait_ge(gram_out_v, before + 1)
                for i in range(GB):
                    at = tl * P + 4 * (kb * GB + i)
                    four = turned[:, par, at:at + 4, :]
                    last = nc.tensor.matmul(ps_gram[kb % 2][:, i * 4 * FM:(i + 1) * 4 * FM],
                                            four.rearrange("d b f -> d (b f)"), four[:, :, 1:F],
                                            start=True, stop=True)
                last.then_inc(gram_ready, 1)

            pe.sem_inc(turn_ready, TURN0)
            pe.sem_inc(hot_used, OH_BUFS)
            pe.wait_ge(const_ready, CONSTS)
            pe.wait_ge(ids_ready, 1)
            first = (0, 0, 0)
            spread_ids(first, 0)
            for s in range(STEPS[0]):
                hot_step(first, s, tables_new=True)
            pe.wait_ge(lo_ready, len(hot))
            pe.wait_ge(pads_ready, 3)
            chunk_step(0, 0, 0, mlp=False)
            pe.wait_ge(w1_ready, KP + 1)
            pe.wait_ge(w_up, 16 * 4)
            with pe.Fori(0, LOOPS) as p:
                for c, par, nth in both(p):
                    chunk_step(c, par, nth)
            chunk_step(CHUNKS - 1, 1, CHUNKS // 2 - 1, False, False)
            for product in mlp_products:
                mlp_product(CHUNKS - 2, *product)
            for product in last_products:
                mlp_product(CHUNKS - 1, *product)

        @block_.scalar
        def _(act):
            def copy(dst, src):
                return nc.scalar.activation(dst, src, ACT.Copy)

            def take_ids(h, u):
                act.wait_ge(ids_spread, units_before(h) + u + 1)
                if u > 1 or not is_first(h[0]):
                    act.wait_ge(hot_ready, CK * (units_before(h) + u - 1))
                nc.scalar.activation(ids_buffer(h[1], u), ps_ids[:, 0:len(units[h[1]][u]), :],
                                     ACT.Copy).then_inc(ids_out, 1)

            def take_lookups(h, u):
                act.wait_ge(hot_used, OH_BUFS + CK * (units_before(h) + u + 1))
                for n, t in enumerate(units[h[1]][u]):
                    last = nc.scalar.activation(turned[:, h[1], :, t + 1], ps_hot[:, n, :], ACT.Copy)
                last.then_inc(look_out, 1)

            def hot_step(h, s):
                u, step = divmod(s, CK)
                if step == SPREAD_AT:
                    if u + 1 < UNITS[h[1]]:
                        take_ids(h, u + 1)
                    else:
                        take_ids(after(h), 0)
                if step == CK - 1:
                    take_lookups(h, u)

            def take_gram(c, par, nth, tl, kb):
                act.wait_ge(gram_ready, GBANKS * (TILES * c + tl) + kb + 1)
                if tl == 0 and kb == 0 and not (isinstance(nth, int) and nth == 0):
                    act.wait_ge(gram_stored, 16 * (c - 1))
                    act.wait_ge(again_stored, 16 * (c - 1))
                for j in ACT_QUADS:
                    last = nc.scalar.activation(gram_dst(par, tl, kb, j), gram_src(kb, j), ACT.Copy)
                last.then_inc(gram_out_a, 1)

            def take_mlp(c, layer, m, k):
                if not last_of_group(layer, k):
                    return
                g, ps = group_index(layer, m), mlp_bank(c, layer, m)
                act.wait_ge(mlp_ready, MLP_GROUPS * c + g + 1)
                if layer == 1:
                    if m == 0 and not is_first(c):
                        act.wait_ge(y_stored, 16 * c)
                    nc.scalar.activation(h1[:, m, :], ps[:], ACT.Relu, bias=bias1[:, m:m + 1]).then_inc(mlp_out, 1)
                elif layer == 2:
                    nc.scalar.activation(h2_of(c)[:, m, :], ps[:], ACT.Relu, bias=bias2[:, m:m + 1]).then_inc(mlp_out, 1)
                else:
                    nc.scalar.activation(y.rearrange("o (l i j) -> o j l i", j=4, l=TILES),
                                         ps[0:1, :].rearrange("o (j l i) -> o j l i", j=4, l=TILES),
                                         ACT.Copy).then_inc(mlp_out, 1)

            def split_input(c, par):
                act.wait_ge(pairs_up, 16 * NREAD * (c + 1))
                for to, of in input_parts(x_hi, par):
                    last = nc.scalar.activation(to, of, ACT.Copy)
                last.then_inc(x_hi_ready, 1)

            def split_slice(k):
                for eng, lines in enumerate(last_reads if k != KD else []):
                    act.wait_ge(last_up[eng][k], 16 * sum(line[3] == k for line in lines))
                to, of = input_slice(x_hi, (CHUNKS - 1) % 2, k)
                nc.scalar.activation(to, of, ACT.Copy).then_inc(x_hi_ready, 1)

            def split_w1(k, of):
                if k != KD:
                    act.wait_ge(w1_up[k], 16)
                else:
                    act.wait_ge(w1_added, 1)
                rows_k = slice_rows(k)
                nc.scalar.activation(w1_hi[0:rows_k, k, :], of[0:rows_k, :], ACT.Copy).then_inc(w1_hi_ready, 1)

            def chunk_step(c, par, nth, mlp=True, hot_next=True):
                for tl, place in places_of(c):
                    kind, n = place
                    if kind == "gram":
                        take_gram(c, par, nth, tl, n)
                    elif not turned_by_dve(c, tl, n):
                        act.wait_ge(turn_ready, TURN0 + NGRP * (TILES * c + tl) + n + 1)
                        take_turned(copy, par, tl, n).then_inc(turn_out, 1)
                    if is_first(c) and (tl, place) in w1_places:
                        split_w1(*w1_slices[w1_places.index((tl, place))])
                    if not is_first(c) and (tl, place) == (LAST_SPLIT_AFTER if is_last(c) else SPLIT_AFTER):
                        split_input(c - 1, 1 - par)
                    if hot_next:
                        for s in hot_at(1 - par, tl, place):
                            hot_step(after((c, par, nth)), s)
                    if mlp:
                        for product in mlp_at(tl, place):
                            take_mlp(c - 1, *product)

            act.sem_inc(turn_out, 2)
            act.sem_inc(look_out, 1)
            act.sem_inc(mlp_out, 1)
            act.sem_inc(gram_out_a, 2)

            first = (0, 0, 0)
            take_ids(first, 0)
            for s in range(STEPS[0]):
                for n, t in enumerate(hot):
                    if s == max(n // PAIRED - 1, 0) * CK:
                        act.wait_ge(stage_up[n % STAGES], 16 * (n // STAGES + 1))
                        nc.scalar.activation(tab_hi[0:VP, n, :, :],
                                             stage[n % STAGES].rearrange("p (c d) -> p c d", c=CK),
                                             ACT.Copy).then_inc(hi_ready, 1)
                hot_step(first, s)
            chunk_step(0, 0, 0, mlp=False)
            with act.Fori(0, LOOPS) as p:
                for c, par, nth in both(p):
                    chunk_step(c, par, nth)
            chunk_step(CHUNKS - 1, 1, CHUNKS // 2 - 1, False, False)
            for product in mlp_products:
                take_mlp(CHUNKS - 2, *product)
                if product == (1, M1 - 1, KP - 1):
                    split_slice(KD)
            for k in range(KP):
                split_slice(k)
            for product in last_products:
                take_mlp(CHUNKS - 1, *product)

        @block_.vector
        def _(dve):
            def make_hot(h, s):
                par, (u, step) = h[1], divmod(s, CK)
                if step == 0:
                    dve.wait_ge(ids_out, units_before(h) + u + 1)
                dve.wait_ge(hot_used, CK * units_before(h) + s + 1)
                nc.vector.tensor_scalar(onehot[0:VP, s % OH_BUFS, 0:len(units[par][u]), :], ids_buffer(par, u)[0:VP],
                                        row_no[0:VP, step:step + 1], None, ALU.is_equal).then_inc(hot_ready, 1)

            def take_gram(c, par, nth, tl, kb):
                dve.wait_ge(gram_ready, GBANKS * (TILES * c + tl) + kb + 1)
                if tl == 0 and kb == 0 and not (isinstance(nth, int) and nth == 0):
                    dve.wait_ge(gram_stored, 16 * (c - 1))
                    dve.wait_ge(again_stored, 16 * (c - 1))
                for j in DVE_QUADS:
                    last = nc.vector.tensor_copy(gram_dst(par, tl, kb, j), gram_src(kb, j))
                last.then_inc(gram_out_v, 1)

            def split_input(c, par):
                dve.wait_ge(x_hi_ready, c + 1)
                for (to, of), (hi, _) in zip(input_parts(x_lo, par), input_parts(x_hi[:].bitcast(F32), par)):
                    last = nc.vector.tensor_tensor(to, of, hi, ALU.subtract)
                last.then_inc(x_ready, 1)

            def prepare_w1(place):
                if place == w1_add_after:
                    dve.wait_ge(w1_dense_up, 32)
                    nc.vector.tensor_tensor(w1_dense, w1_dense, w1_again, ALU.add).then_inc(w1_added, 1)
                if place in w1_places:
                    n = w1_places.index(place)
                    k, of = w1_slices[n]
                    dve.wait_ge(w1_hi_ready, n + 1)
                    rows_k = slice_rows(k)
                    nc.vector.tensor_tensor(w1_lo[0:rows_k, k, :], of[0:rows_k, :],
                                            w1_hi[0:rows_k, k, :].bitcast(F32), ALU.subtract).then_inc(w1_ready, 1)

            def chunk_step(c, par, nth, hot_next=True):
                for tl, place in places_of(c):
                    kind, n = place
                    if kind == "turn" and turned_by_dve(c, tl, n):
                        dve.wait_ge(turn_ready, TURN0 + NGRP * (TILES * c + tl) + n + 1)
                        take_turned(nc.vector.tensor_copy, par, tl, n).then_inc(turn_out_v, 1)
                    if hot_next:
                        for s in hot_at(1 - par, tl, place, HOT_AHEAD):
                            make_hot(after((c, par, nth)), s)
                    if kind == "gram":
                        take_gram(c, par, nth, tl, n)
                    if is_first(c):
                        prepare_w1((tl, place))
                    elif (tl, place) == (LAST_SPLIT_AFTER if is_last(c) else SPLIT_AFTER):
                        split_input(c - 1, 1 - par)

            dve.sem_inc(gram_out_v, 2)
            nc.vector.memset(ids_f[:].bitcast(F32), 0.0).then_inc(pads_ready, 1)
            dve.wait_ge(pads_ready, 1)
            dve.wait_ge(ids_up, 16)
            nc.vector.tensor_scalar(ids_f[0:len(tables), 0:B], ids_in, 2047.0, None, ALU.min).then_inc(ids_ready, 1)
            dve.wait_ge(ids_ready, 1)
            for par in range(2):
                nc.vector.memset(turned[:, par, :, F:QUAD], 0.0).then_inc(pads_ready, 1)
            dve.wait_ge(const_ready, CONSTS)
            nc.vector.tensor_copy(row_no[:], row_no_i[:]).then_inc(row_no_ready, 1)
            dve.wait_ge(row_no_ready, 1)

            def low_part(n):
                dve.wait_ge(hi_ready, n + 1)
                nc.vector.tensor_tensor(tab_lo[0:VP, n, :, :], stage[n % STAGES].rearrange("p (c d) -> p c d", c=CK),
                                        tab_hi[0:VP, n, :, :].bitcast(F32), ALU.subtract).then_inc(lo_ready, 1)

            for s in range(STEPS[0]):
                if s % CK == 0:
                    for n in range(len(units[0][s // CK])):
                        low_part(s // CK * PAIRED + n)
                make_hot((0, 0, 0), s)
            for n in range(len(hot_of[0]), len(hot)):
                low_part(n)
            chunk_step(0, 0, 0)
            with dve.Fori(0, LOOPS) as p:
                for c, par, nth in both(p):
                    chunk_step(c, par, nth)
            chunk_step(CHUNKS - 1, 1, CHUNKS // 2 - 1, hot_next=False)
            for n, k in enumerate(slices):
                dve.wait_ge(x_hi_ready, CHUNKS + n)
                to, of = input_slice(x_lo, 1, k)
                nc.vector.tensor_tensor(to, of, input_slice(x_hi[:].bitcast(F32), 1, k)[0],
                                        ALU.subtract).then_inc(x_ready, 1)


_TABLES = [f"tbl_{n}" for n in range(26)]
_INS = ["r_dense_output", "ids", "W_top1", "b_top1", "W_top2", "b_top2", "W_top3"] + _TABLES


def kernel(**inputs):
    import numpy as _np
    import concourse.bacc as _bacc
    from concourse import mybir as _mybir
    from concourse.bass_utils import run_bass_kernel_spmd as _run

    nc = _bacc.Bacc("TRN2", target_bir_lowering=False, num_devices=1)
    arrays, aps = {}, {}
    given = {name: inputs[name] for name in _INS}
    given["ids_t"] = _np.asarray(inputs["ids"]).T
    w1, dim, sparse = _np.asarray(inputs["W_top1"]), inputs["r_dense_output"].shape[1], len(_TABLES)
    number = {pair: n for n, pair in enumerate((f, g) for f in range(sparse + 1) for g in range(f + 1, sparse + 1))}
    order = [number[pair] for pair in pair_list(sparse, len(number) // -(-len(number) // P))]
    given["W_top1"] = _np.concatenate([w1[:dim], w1[dim:-dim][order], w1[-dim:]])
    for name, value in given.items():
        a = _np.ascontiguousarray(value)
        arrays[f"in_{name}"] = a
        aps[name] = nc.dram_tensor(f"in_{name}", a.shape, _mybir.dt.from_np(a.dtype), kind="ExternalInput").ap()
    rows, dt = aps["ids"].shape[0], _mybir.dt.float32
    out = nc.dram_tensor("out", (rows, 1), dt, kind="ExternalOutput").ap()
    scratch = nc.dram_tensor("gram_scratch", (rows // CHUNK, 4, QUAD * (len(_TABLES) * 3 // 2 - 1), CHUNK // 4), dt, kind="Internal").ap()
    build(nc, aps["r_dense_output"], aps["ids"], aps["ids_t"], [aps[t] for t in _TABLES], aps["W_top1"],
          aps["b_top1"], aps["W_top2"], aps["b_top2"], aps["W_top3"], scratch, out)
    r = _run(nc, [arrays], core_ids=[0])
    return r.results[0]["out"]
```
